# Optimizing a Trainium2 kernel written in Bass

```python
import numpy as np
import jax
import jax.numpy as jnp

def _softmax(x, axis=-1):
    return jax.nn.softmax(x, axis=axis)

def _gelu(x):
    return jax.nn.gelu(x, approximate=True)

def _silu(x):
    return jax.nn.silu(x)

def _sigmoid(x):
    return jax.nn.sigmoid(x)

def _layernorm(x, axis=-1, eps=1e-05):
    m = jnp.mean(x, axis=axis, keepdims=True)
    v = jnp.var(x, axis=axis, keepdims=True)
    return (x - m) / jnp.sqrt(v + eps)

def _scatter_add(tgt, idx, src, axis=0):
    return tgt.at[idx].add(src)

def _segment_sum(src, seg, n):
    return jax.ops.segment_sum(src, seg, n)
kernel_name = 'mk_flamingo_gated_d1_seqx_r8_3b58e6'

def setup_inputs(seed: int=0):
    np.random.seed(seed)
    _w = jnp.asarray

    def _rec_inputs():
        import jax
        import jax.numpy as jnp
        _rk = jax.random.key(seed)
        x = 7.22e-05 + 1 * jax.random.normal(jax.random.fold_in(_rk, 1), (8, 128, 512), jnp.float32)
        _lenS = 128 - jax.random.randint(jax.random.fold_in(_rk, 7), (8,), 0, max(1, 128 // 4) + 1, jnp.int32)
        _lenS2 = 128 - jax.random.randint(jax.random.fold_in(_rk, 8), (8,), 0, max(1, 128 // 4) + 1, jnp.int32)
        _ctx_4096P = jax.random.normal(jax.random.fold_in(_rk, 11), (8, 16, 512), jnp.float32)
        _ctx_4096c = jax.random.dirichlet(jax.random.fold_in(_rk, 511), 0.3 * jnp.ones((16,), jnp.float32), (8, 128))
        _ctx_4096t = jnp.einsum('bsk,bkd->bsd', _ctx_4096c, _ctx_4096P)
        _ctx_4096t = _ctx_4096t * jax.lax.rsqrt(jnp.mean(jnp.square(_ctx_4096t)) + 1e-12) * 0.953939
        ctx_4096 = 4.13588e-05 + 0.999923 * (_ctx_4096t + 0.3 * jax.random.normal(jax.random.fold_in(_rk, 611), (8, 128, 512), jnp.float32))
        _validS = jnp.arange(128)[None, :] < _lenS[:, None]
        _validS2 = jnp.arange(128)[None, :] < _lenS2[:, None]
        _causal = jnp.tril(jnp.ones((128, 128), dtype=bool))
        mask_BxSxS2_bk0 = jnp.logical_not(jnp.broadcast_to(_validS2[:, None, :], (8, 128, 128)))
        _g = jax.random.normal(jax.random.fold_in(_rk, 9001), (2, 1), jnp.float32)
        _g = jnp.sign(_g) * jnp.maximum(jnp.abs(_g), 1.0) + (_g == 0) * 1.0
        g_xattn = _g[0]
        g_ffn = _g[1]
        return (x, ctx_4096, mask_BxSxS2_bk0, g_xattn, g_ffn)
    x, ctx_4096, mask_BxSxS2_bk0, g_xattn, g_ffn = _rec_inputs()

    def _L0_xattn_setup():
        import jax, jax.numpy as jnp
        import numpy as np
        B, LQ, LK, D, H, DH = (2, 128, 128, 512, 32, 128)
        EPS = 1e-05

        def _rmsnorm(x, weight):
            var = jnp.mean(jnp.square(x), axis=-1, keepdims=True)
            return x * jax.lax.rsqrt(var + EPS) * weight
        key = jax.random.key(seed)
        ks = jax.random.split(key, 8)
        scale = 0.02
        return {'hidden_states': jax.random.normal(ks[0], (B, LQ, D), jnp.float32), 'key_value_states': jax.random.normal(ks[1], (B, LK, D), jnp.float32), 'attention_mask': jax.random.randint(ks[2], (B, LQ, LK), 0, 2) > 0, 'position_bias': jax.random.normal(ks[3], (H, LQ, LK), jnp.float32), 'ln_weight': jnp.ones((D,), jnp.float32), 'w_q': jax.random.normal(ks[4], (H * DH, D), jnp.float32) * scale, 'w_k': jax.random.normal(ks[5], (H * DH, D), jnp.float32) * scale, 'w_v': jax.random.normal(ks[6], (H * DH, D), jnp.float32) * scale, 'w_out': jax.random.normal(ks[7], (D, H * DH), jnp.float32) * scale}
    _L0_xattn_all = _L0_xattn_setup()
    _L0_xattn_in = {k: v for k, v in _L0_xattn_all.items() if k in ('position_bias', 'ln_weight', 'w_q', 'w_k', 'w_v', 'w_out')}
    del _L0_xattn_all

    def _L0_ffn_setup():
        import jax, jax.numpy as jnp
        import numpy as np
        N_EXPERTS = 28
        TOP_K = 2
        RANK = 8
        LORA_ALPHA = 16
        SCALING = LORA_ALPHA / RANK
        TEMP = 1.0
        key = jax.random.key(seed)
        ks = jax.random.split(key, 5)
        B, S, D_IN, D_OUT = (4, 256, 512, 512)
        x = jax.random.normal(ks[0], (B, S, D_IN), dtype=jnp.float32)
        base_W = jax.random.normal(ks[1], (D_OUT, D_IN), dtype=jnp.float32) * (1.0 / np.sqrt(D_IN))
        gate_W = jax.random.normal(ks[2], (N_EXPERTS, D_IN), dtype=jnp.float32) * (1.0 / np.sqrt(D_IN))
        lora_A = jax.random.normal(ks[3], (N_EXPERTS, RANK, D_IN), dtype=jnp.float32) * (1.0 / np.sqrt(D_IN))
        lora_B = jax.random.normal(ks[4], (N_EXPERTS, D_OUT, RANK), dtype=jnp.float32) * 0.01
        return {'x': x, 'base_W': base_W, 'gate_W': gate_W, 'lora_A': lora_A, 'lora_B': lora_B}
    _L0_ffn_all = _L0_ffn_setup()
    _L0_ffn_in = {k: v for k, v in _L0_ffn_all.items() if k in ('base_W', 'gate_W', 'lora_A', 'lora_B')}
    del _L0_ffn_all
    return {'x': x, 'ctx_4096': ctx_4096, 'mask_BxSxS2_bk0': mask_BxSxS2_bk0, 'g_xattn': g_xattn, 'g_ffn': g_ffn, 'L0_xattn_position_bias': _L0_xattn_in['position_bias'], 'L0_xattn_ln_weight': _L0_xattn_in['ln_weight'], 'L0_xattn_w_q': _L0_xattn_in['w_q'], 'L0_xattn_w_k': _L0_xattn_in['w_k'], 'L0_xattn_w_v': _L0_xattn_in['w_v'], 'L0_xattn_w_out': _L0_xattn_in['w_out'], 'L0_ffn_base_W': _L0_ffn_in['base_W'], 'L0_ffn_gate_W': _L0_ffn_in['gate_W'], 'L0_ffn_lora_A': _L0_ffn_in['lora_A'], 'L0_ffn_lora_B': _L0_ffn_in['lora_B']}

def reference(x, ctx_4096, mask_BxSxS2_bk0, g_xattn, g_ffn, L0_xattn_position_bias, L0_xattn_ln_weight, L0_xattn_w_q, L0_xattn_w_k, L0_xattn_w_v, L0_xattn_w_out, L0_ffn_base_W, L0_ffn_gate_W, L0_ffn_lora_A, L0_ffn_lora_B):
    import jax
    import jax.numpy as jnp

    def _L0_xattn_ref(hidden_states, key_value_states, attention_mask, position_bias, ln_weight, w_q, w_k, w_v, w_out):
        import jax, jax.numpy as jnp
        import numpy as np
        B, LQ, LK, D, H, DH = (2, 128, 128, 512, 32, 128)
        EPS = 1e-05

        def _rmsnorm(x, weight):
            var = jnp.mean(jnp.square(x), axis=-1, keepdims=True)
            return x * jax.lax.rsqrt(var + EPS) * weight
        x = _rmsnorm(hidden_states, ln_weight)
        b, lq, _ = x.shape
        lk = key_value_states.shape[1]
        h_q = (x @ w_q.T).reshape(b, lq, H, DH)
        h_k = (key_value_states @ w_k.T).reshape(b, lk, H, DH)
        h_v = (key_value_states @ w_v.T).reshape(b, lk, H, DH)
        score = jnp.einsum('bqhd,bkhd->bhqk', h_q, h_k)
        score = score + position_bias[None]
        m = attention_mask[:, None]
        score = jnp.where(m, score, -jnp.inf)
        score = jax.nn.softmax(score, axis=-1)
        score = jnp.where(m, score, 0.0)
        attn = jnp.einsum('bhqk,bkhd->bqhd', score, h_v).reshape(b, lq, H * DH)
        out = attn @ w_out.T
        return hidden_states + out

    def _L0_ffn_ref(x, base_W, gate_W, lora_A, lora_B):
        import jax, jax.numpy as jnp
        import numpy as np
        N_EXPERTS = 28
        TOP_K = 2
        RANK = 8
        LORA_ALPHA = 16
        SCALING = LORA_ALPHA / RANK
        TEMP = 1.0
        B, S, D_in = x.shape
        xf = x.reshape(B * S, D_in)
        base = xf @ base_W.T
        logits = xf @ gate_W.T
        top_vals, top_idx = jax.lax.top_k(logits, TOP_K)
        top_probs = jax.nn.softmax(top_vals / TEMP, axis=-1)
        N = xf.shape[0]
        gate_full = jnp.zeros((N, N_EXPERTS), dtype=xf.dtype).at[jnp.arange(N)[:, None], top_idx].add(top_probs)
        h = jnp.einsum('nd,erd->ner', xf, lora_A)
        h = h * (gate_full * SCALING)[:, :, None]
        lora_out = jnp.einsum('ner,eor->no', h, lora_B)
        out = base + lora_out
        return out.reshape(B, S, -1)
    x = x + jnp.tanh(g_xattn[0]) * _L0_xattn_ref(_layernorm(x, axis=-1), ctx_4096, mask_BxSxS2_bk0, L0_xattn_position_bias, L0_xattn_ln_weight, L0_xattn_w_q, L0_xattn_w_k, L0_xattn_w_v, L0_xattn_w_out)
    x = x + jnp.tanh(g_ffn[0]) * _L0_ffn_ref(_layernorm(x, axis=-1), L0_ffn_base_W, L0_ffn_gate_W, L0_ffn_lora_A, L0_ffn_lora_B)
    return x

_drawn_inputs = setup_inputs


def setup_inputs(seed=0):
    import zlib

    import numpy as np

    out = dict(_drawn_inputs(seed))
    spreads = {'L0_xattn_ln_weight': (1.0, 0.562)}
    factors = {'L0_ffn_gate_W': 3.194, 'L0_ffn_lora_A': 3.051, 'L0_ffn_lora_B': 3.097}
    for name, (base, spread) in spreads.items():
        noise = np.random.default_rng([zlib.crc32(name.encode()), seed]).standard_normal(out[name].shape)
        drawn = base * np.exp(spread * noise) if base else spread * noise
        out[name] = jnp.asarray(drawn.astype(out[name].dtype))
    for name, factor in factors.items():
        out[name] = (out[name] * factor).astype(out[name].dtype)
    return out
```

```python
from contextlib import ExitStack

import concourse.bass as bass
from concourse import mybir

F32 = mybir.dt.float32
F32R = mybir.dt.float32r
U8 = mybir.dt.uint8
U32 = mybir.dt.uint32
ALU = mybir.AluOpType
ACT = mybir.ActivationFunctionType
AX = mybir.AxisListType

P = 128
B, S, D = 8, 128, 512
H, DH = 32, 128
E, R, TOP = 28, 8, 2
SCALING = 16 / R
EPS = 1e-5
NEG = -1e30
T = B * S
C = D // P
HP = 2
NPH = H // HP
HALF = T // 2
UNITS = HP * 2
BU = B // 2
QK = 2 * UNITS
VC = B // 2
PROJ = QK + VC
BANKS = 4
WQ, WK, WV, WO = range(4)
WN = C * HP * DH
ER = E * R
ERH = ER // 2
LG = 256


def build(nc, x, ctx_t, weights, bias, mask, g_x, g_f, ln_w, out):
    ctx = ExitStack()
    with ctx:
        def sb(name, shape, dt=F32):
            return ctx.enter_context(nc.sbuf_tensor(name, shape, dt))

        def sem(name):
            return ctx.enter_context(nc.semaphore(name))

        def bank(name):
            return ctx.enter_context(nc.psum_tensor(name, [P, 512], F32))

        xt_hi, xt_lo = sb("xt_hi", [P, C, T], F32R), sb("xt_lo", [P, C, T], F32R)
        ct_hi, ct_lo = sb("ct_hi", [P, C, T], F32R), sb("ct_lo", [P, C, T], F32R)
        w_hi, w_lo = sb("w_hi", [P, 4, WN], F32R), sb("w_lo", [P, 4, WN], F32R)
        w_raw = sb("w_raw", [P, 4, WN])
        qt, kt = sb("qt", [P, HP, T]), sb("kt", [P, HP, T])
        v_sb = sb("v_sb", [P, B, HP * DH])
        at_hi, at_lo = sb("at_hi", [P, HP, T], F32R), sb("at_lo", [P, HP, T], F32R)
        acc = sb("acc", [P, B, D])
        bias_sb = sb("bias_sb", [P, HP, S])
        comb = sb("comb", [P, HP, B, S])
        mask_u8 = sb("mask_u8", [P, B, S], U8)
        mask_add = sb("mask_add", [P, B, S])
        row_any = sb("row_any", [P, B])
        probs = sb("probs", [P, 2, BU, S])
        probs_t = sb("probs_t", [P, BU, S])
        neg_max, row_sum, row_scale = (sb(n, [P, UNITS, BU]) for n in ("neg_max", "row_sum", "row_scale"))
        ident = sb("ident", [P, P])
        lnw = sb("lnw", [P, D])
        gates = sb("gates", [P, 2])
        tanh_g = sb("tanh_g", [P, 2])
        stats = sb("stats", [P, B, 6])
        mean_var = sb("mean_var", [P, B, 2])
        pow_half = sb("pow_half", [P, B])
        var_e, rstd, newton = sb("var_e", [P, B]), sb("rstd", [P, B]), sb("newton", [P, B])
        sum_sq = sb("sum_sq", [P, B])
        expert_id = sb("expert_id", [P, E])
        top_v, top_i, top_f = sb("top_v", [P, 2, 8]), sb("top_i", [P, 2, 8], U32), sb("top_f", [P, 2, 8])
        gap, e_gap, gate1, gate2 = (sb(n, [P, B]) for n in ("gap", "e_gap", "gate1", "gate2"))
        pick1, pick2 = sb("pick1", [P, 2, E]), sb("pick2", [P, 2, E])
        hg = sb("hg", [P, 2, ER])
        hgt_hi, hgt_lo = sb("hgt_hi", [ERH, 2, 2, P], F32R), sb("hgt_lo", [ERH, 2, 2, P], F32R)
        result = sb("result", [P, 2, D])

        score_ps = [bank(f"score_ps{i}") for i in range(2)]
        turn_ps, pv_ps = bank("turn_ps"), bank("pv_ps")
        proj_ps = [bank(f"proj_ps{i}") for i in range(BANKS)]

        ctx_raw = [t[:, i, :] for t in (qt, kt) for i in range(HP)]
        xn = v_sb[:, :, :].rearrange("p (i n) d -> p i (n d)", n=2)
        x_again = [t[:, i // 2, (i % 2) * D:(i % 2 + 1) * D] for t in (qt, kt) for i in range(B // 2)]
        base_w = [w[:, 0:2, :].rearrange("p a (c n) -> p (a c) n", n=D) for w in (w_hi, w_lo)]
        lg_w = [w[:, 2, :].rearrange("p (c n) -> p c n", n=LG) for w in (w_hi, w_lo)]
        lb_w = [w[0:ERH, 3, :].rearrange("p (e n) -> p e n", n=D) for w in (w_hi, w_lo)]

        x_in = [sem(f"x_in{i}") for i in range(4)]
        ctx_in = [sem(f"ctx_in{i}") for i in range(C)]
        w_in = [sem(f"w_in{k}") for k in range(4)]
        bias_in, mask_in, small_in, x2_in = sem("bias_in"), sem("mask_in"), sem("small_in"), sem("x2_in")
        stored = [sem(f"stored{i}") for i in range(2)]
        w_hi_done = [sem(f"w_hi_done{k}") for k in range(4)]
        w_lo_done = [sem(f"w_lo_done{k}") for k in range(4)]
        ctx_hi_done, ctx_lo_done = sem("ctx_hi_done"), sem("ctx_lo_done")
        ident_zero, ident_done, pow_const, ids_done = sem("ident_zero"), sem("ident_done"), sem("pow_const"), sem("ids_done")
        dve_step = sem("dve_step")
        var_done, rstd0_done = sem("var_done"), sem("rstd0_done")
        sq_done, xn_done, xt_turned = sem("sq_done"), sem("xn_done"), sem("xt_turned")
        xt_hi_done, xt_lo_done = sem("xt_hi_done"), sem("xt_lo_done")
        acc_done = sem("acc_done")
        mask_done, comb_done, tanh_done = sem("mask_done"), sem("comb_done"), sem("tanh_done")
        proj_done, proj_copied = sem("proj_done"), sem("proj_copied")
        scores_done, biased, max_done = sem("scores_done"), sem("biased"), sem("max_done")
        exp_done, scaled, probs_done = sem("exp_done"), sem("scaled"), sem("probs_done")
        turned, turn_copied = sem("turned"), sem("turn_copied")
        pv_done, at_hi_done, at_split = sem("pv_done"), sem("at_hi_done"), sem("at_split")
        out_done = sem("out_done")
        xf_done, xf_turned, xf_hi_done, xf_lo_done = sem("xf_done"), sem("xf_turned"), sem("xf_hi_done"), sem("xf_lo_done")
        logits_done, gap_done, e_gap_done = sem("logits_done"), sem("gap_done"), sem("e_gap_done")
        hg_done, hg_turned, hg_hi_done, hg_lo_done = sem("hg_done"), sem("hg_turned"), sem("hg_hi_done"), sem("hg_lo_done")
        ffn_done, final_done = sem("ffn_done"), sem("final_done")

        block = ctx.enter_context(nc.Block())

        @block.sync
        def _(sp):
            def load_w(k, p):
                sp.dma_start(w_raw[:, k, :], weights[p, k] if isinstance(p, int)
                             else weights[bass.ds(p, 1), k].rearrange("a p n -> p (a n)")).then_inc(w_in[k], 16)

            load_w(WK, 0)
            for c in range(C):
                sp.dma_start(ctx_raw[c], ctx_t[c]).then_inc(ctx_in[c], 16)
            load_w(WV, 0)
            load_w(WQ, 0)
            sp.dma_start(mask_u8[:, :, :], mask.rearrange("b q k -> q b k")).then_inc(mask_in, 16)
            sp.dma_start(bias_sb[:, :, :], bias[0]).then_inc(bias_in, 16)
            load_w(WO, 0)

            def refill(p):
                for k in (WQ, WK, WV):
                    sp.wait_ge(w_lo_done[k], p + 1)
                    load_w(k, p + 1)

            def refill_out(p):
                sp.wait_ge(w_lo_done[WO], p + 1)
                load_w(WO, p + 1)

            with sp.Fori(0, NPH - 1) as p:
                refill(p)
                sp.wait_ge(comb_done, p * HP + HP)
                sp.dma_start(bias_sb[:, :, :], bias[bass.ds(p + 1, 1)].rearrange("a q h k -> q (a h) k")).then_inc(bias_in, 16)
                refill_out(p)
            refill(NPH - 1)
            refill_out(NPH - 1)
            sp.wait_ge(scores_done, UNITS * NPH)
            for i in range(B):
                sp.dma_start(x_again[i], x[i]).then_inc(x2_in, 16)
            for i in range(B):
                sp.wait_ge(final_done, i + 1)
                sp.dma_start(out[i], result[:, i % 2, :]).then_inc(stored[i % 2], 16)
            for s in stored:
                sp.wait_ge(s, 16 * (B // 2))

        @block.gpsimd
        def _(pool):
            pool.memset(ident[:, :], 0.0).then_inc(ident_zero, 1)
            pool.wait_ge(ident_zero, 1)
            pool.affine_select(out=ident[:, :], in_=ident[:, :], compare_op=ALU.not_equal, fill=1.0, base=0,
                               pattern=[[-1, P]], channel_multiplier=1).then_inc(ident_done, 1)
            pool.memset(pow_half[:, :], -0.5).then_inc(pow_const, 1)
            pool.iota(expert_id[:, :], pattern=[[1, E]], base=0, channel_multiplier=0,
                      allow_small_or_imprecise_dtypes=True).then_inc(ids_done, 1)

            def rest(k, p):
                pool.wait_ge(w_hi_done[k], p + 1)
                pool.tensor_tensor(w_lo[:, k, :], w_raw[:, k, :], w_hi[:, k, :].bitcast(F32),
                                   ALU.subtract).then_inc(w_lo_done[k], 1)

            def add_mask(p, first):
                pool.wait_ge(bias_in, (p + 1) * 16)
                for j in range(HP):
                    if not first:
                        pool.wait_ge(biased, (p - 1) * UNITS + (2 * j + 2))
                    pool.tensor_tensor(comb[:, j, :, :], mask_add[:, :, :],
                                       bias_sb[:, j:j + 1, :].to_broadcast([P, B, S]), ALU.add).then_inc(comb_done, 1)

            def inverse_root(n, lo, hi):
                pool.wait_ge(var_done, n)
                pool.tensor_tensor(rstd[:, lo:hi], var_e[:, lo:hi], pow_half[:, lo:hi], ALU.pow).then_inc(rstd0_done, 1)

            rest(WK, 0)
            pool.wait_ge(pow_const, 1)
            inverse_root(1, 0, B)
            rest(WV, 0)
            inverse_root(2, 0, B)
            rest(WQ, 0)
            pool.wait_ge(mask_done, 1)
            add_mask(0, True)
            for k in (WQ, WK, WV):
                rest(k, 1)
            rest(WO, 0)
            with pool.Fori(1, NPH) as p:
                add_mask(p, False)
                for k in (WQ, WK, WV):
                    rest(k, p + 1)
                rest(WO, p)
            for i in range(B):
                inverse_root(3 + i, i, i + 1)
                if i == 0:
                    rest(WO, NPH)

        @block.scalar
        def _(act):
            for i in range(4):
                act.dma_start(acc[:, 2 * i:2 * i + 2, :], x[2 * i:2 * i + 2].rearrange("b s d -> s b d")).then_inc(x_in[i], 16)
            act.dma_start(lnw[:, :], ln_w.rearrange("(a n) -> a n", a=1).to_broadcast([P, D])).then_inc(small_in, 16)
            act.dma_start(gates[:, 0:1], g_x.rearrange("(a n) -> a n", a=1).to_broadcast([P, 1])).then_inc(small_in, 16)
            act.dma_start(gates[:, 1:2], g_f.rearrange("(a n) -> a n", a=1).to_broadcast([P, 1])).then_inc(small_in, 16)

            def lead(k, p):
                act.wait_ge(w_in[k], (p + 1) * 16)
                act.activation(w_hi[:, k, :], w_raw[:, k, :], ACT.Copy).then_inc(w_hi_done[k], 1)

            def copy_proj(p, n, i, dst):
                act.wait_ge(proj_done, p * PROJ + (n + 1))
                act.activation(dst, proj_ps[i][:, :], ACT.Copy).then_inc(proj_copied, 1)

            def q_or_k(m):
                u, t = m // 2, (qt, kt)[m % 2]
                return t[:, u // 2, (u % 2) * HALF:(u % 2 + 1) * HALF]

            def v_dst(m):
                return v_sb[:, 2 * m:2 * m + 2, :].rearrange("p b d -> p (b d)")

            def exps(a, u):
                act.wait_ge(max_done, a * UNITS + (u + 1))
                for i in range(BU):
                    e = act.activation(probs[:, u % 2, i, :], probs[:, u % 2, i, :], ACT.Exp,
                                       bias=neg_max[:, u, i:i + 1], accum_out=row_sum[:, u, i:i + 1])
                e.then_inc(exp_done, 1)

            def lead_at(a, u):
                act.wait_ge(pv_done, a * UNITS + (u + 1))
                act.activation(at_hi[:, u // 2, (u % 2) * HALF:(u % 2 + 1) * HALF], pv_ps[:, :],
                               ACT.Copy).then_inc(at_hi_done, 1)

            lead(WK, 0)
            for c in range(C):
                act.wait_ge(ctx_in[c], 16)
                act.activation(ct_hi[:, c, :], ctx_raw[c], ACT.Copy).then_inc(ctx_hi_done, 1)
            lead(WV, 0)
            for i in range(B):
                act.wait_ge(acc_done, i + 1)
                if i:
                    act.wait_ge(sq_done, i)
                act.activation(probs_t[:, :, :].rearrange("p b s -> p (b s)"), acc[:, i, :], ACT.Square,
                               accum_out=sum_sq[:, i:i + 1]).then_inc(sq_done, 1)
            lead(WQ, 0)
            act.wait_ge(small_in, 48)
            act.activation(tanh_g[:, :], gates[:, :], ACT.Tanh).then_inc(tanh_done, 1)
            for m in range(UNITS):
                copy_proj(0, m, m % BANKS, q_or_k(2 * m + 1))
            for i in range(B):
                act.wait_ge(xt_turned, i + 1)
                act.activation(xt_hi[:, :, i * P:(i + 1) * P], score_ps[i % 2][:, :].rearrange("p (c s) -> p c s", c=C),
                               ACT.Copy).then_inc(xt_hi_done, 1)
            for m in range(VC):
                copy_proj(0, UNITS + m, m % BANKS, v_dst(m))
            for m in range(UNITS):
                copy_proj(0, UNITS + VC + m, m % BANKS, q_or_k(2 * m))
            for k in (WQ, WK, WV):
                lead(k, 1)
            lead(WO, 0)

            def iteration(p, project):
                a = p - 1
                def chunk(n):
                    if project:
                        copy_proj(p, n, n % BANKS, q_or_k(n) if n < QK else v_dst(n - QK))
                exps(a, 0)
                chunk(0)
                exps(a, 1)
                chunk(1)
                chunk(2)
                exps(a, 2)
                lead_at(a, 0)
                chunk(3)
                exps(a, 3)
                lead_at(a, 1)
                for n in (4, 5, 6):
                    chunk(n)
                lead_at(a, 2)
                chunk(7)
                lead_at(a, 3)
                for n in range(QK, PROJ):
                    chunk(n)
                if project:
                    for k in (WQ, WK, WV):
                        lead(k, p + 1)
                act.wait_ge(out_done, p * B)
                lead(WO, p)

            with act.Fori(1, NPH) as p:
                iteration(p, True)
            iteration(NPH, False)

            def lead_xf(i):
                act.wait_ge(xf_turned, i + 1)
                act.activation(xt_hi[:, :, i * P:(i + 1) * P], score_ps[i % 2][:, :].rearrange("p (c s) -> p c s", c=C),
                               ACT.Copy).then_inc(xf_hi_done, 1)

            lead_xf(0)
            for i in range(B):
                act.wait_ge(gap_done, i + 1)
                act.activation(e_gap[:, i:i + 1], gap[:, i:i + 1], ACT.Exp).then_inc(e_gap_done, 1)
                if i + 1 < B:
                    lead_xf(i + 1)
                act.wait_ge(hg_turned, i + 1)
                act.activation(hgt_hi[:, i % 2, :, :], proj_ps[2 + i % 2][0:ERH, 0:2 * P].rearrange("p (e s) -> p e s", e=2),
                               ACT.Copy).then_inc(hg_hi_done, 1)

        @block.vector
        def _(dve):
            steps = [0]

            def ordered(ins):
                steps[0] += 1
                ins.then_inc(dve_step, 1)
                dve.wait_ge(dve_step, steps[0])

            def refine(n, lo, hi):
                r, v, t = rstd[:, lo:hi], var_e[:, lo:hi], newton[:, lo:hi]
                dve.wait_ge(rstd0_done, n)
                ordered(dve.tensor_tensor(t, r, r, ALU.mult))
                ordered(dve.tensor_tensor(t, t, v, ALU.mult))
                ordered(dve.tensor_scalar(t, t, -0.5, 1.5, ALU.mult, ALU.add))
                ordered(dve.tensor_tensor(r, r, t, ALU.mult))

            def rest_ctx(c):
                dve.wait_ge(ctx_hi_done, c + 1)
                dve.tensor_tensor(ct_lo[:, c, :], ctx_raw[c], ct_hi[:, c, :].bitcast(F32), ALU.subtract).then_inc(ctx_lo_done, 1)

            for i in range(B):
                if i % 2 == 0:
                    dve.wait_ge(x_in[i // 2], 16)
                ordered(dve.bn_stats(stats[:, i, :], acc[:, i, :]))
                ordered(dve.bn_aggr(mean_var[:, i, :], stats[:, i, :]))
            dve.tensor_scalar(var_e[:, :], mean_var[:, :, 1], EPS, None, ALU.add).then_inc(var_done, 1)
            for c in range(C):
                rest_ctx(c)
            refine(1, 0, B)
            for i in range(B):
                dve.tensor_scalar(acc[:, i, :], acc[:, i, :], mean_var[:, i, 0:1], rstd[:, i:i + 1],
                                  ALU.subtract, ALU.mult).then_inc(acc_done, 1)
            dve.wait_ge(sq_done, B)
            dve.tensor_scalar(var_e[:, :], sum_sq[:, :], 1.0 / D, EPS, ALU.mult, ALU.add).then_inc(var_done, 1)
            refine(2, 0, B)
            dve.wait_ge(small_in, 48)

            def rest_xt(i, hi_done, lo_done):
                dve.wait_ge(hi_done, i + 1)
                dve.tensor_tensor(xt_lo[:, :, i * P:(i + 1) * P], score_ps[i % 2][:, :].rearrange("p (c s) -> p c s", c=C),
                                  xt_hi[:, :, i * P:(i + 1) * P].bitcast(F32), ALU.subtract).then_inc(lo_done, 1)

            for i in range(B):
                if i >= 4:
                    rest_xt(i - 4, xt_hi_done, xt_lo_done)
                dve.scalar_tensor_tensor(out=xn[:, i % 4, :], in0=acc[:, i, :], scalar=rstd[:, i:i + 1], in1=lnw[:, :],
                                         op0=ALU.mult, op1=ALU.mult).then_inc(xn_done, 1)
            for i in range(4, B):
                rest_xt(i, xt_hi_done, xt_lo_done)
            dve.wait_ge(mask_in, 16)
            dve.tensor_scalar(mask_add[:, :, :], mask_u8[:, :, :], 1.0, -NEG, ALU.subtract, ALU.mult).then_inc(mask_done, 1)
            ordered(dve.tensor_reduce(row_any[:, :], mask_u8[:, :, :], AX.X, ALU.max))

            def add_bias(a, u):
                j, t = u // 2, u % 2
                dve.wait_ge(scores_done, a * UNITS + (u + 1))
                dve.wait_ge(comb_done, a * HP + (j + 1))
                dve.tensor_tensor(probs[:, u % 2, :, :], score_ps[u % 2][:, :].rearrange("p (b s) -> p b s", b=BU),
                                  comb[:, j, t * BU:(t + 1) * BU, :], ALU.add).then_inc(biased, 1)
                dve.wait_ge(biased, a * UNITS + (u + 1))
                dve.tensor_reduce(neg_max[:, u, :], probs[:, u % 2, :, :], AX.X, ALU.max, negate=True).then_inc(max_done, 1)

            def normalise(a, u):
                t = u % 2
                dve.wait_ge(exp_done, a * UNITS + (u + 1))
                dve.reciprocal(row_scale[:, u, :], row_sum[:, u, :]).then_inc(scaled, 1)
                dve.wait_ge(scaled, a * (2 * UNITS) + (2 * u + 1))
                dve.tensor_tensor(row_scale[:, u, :], row_scale[:, u, :], row_any[:, t * BU:(t + 1) * BU],
                                  ALU.mult).then_inc(scaled, 1)
                dve.wait_ge(scaled, a * (2 * UNITS) + (2 * u + 2))
                dve.tensor_tensor(probs[:, u % 2, :, :], probs[:, u % 2, :, :],
                                  row_scale[:, u, :].unsqueeze(2).to_broadcast([P, BU, S]), ALU.mult).then_inc(probs_done, 1)

            def copy_turned(a, u):
                dve.wait_ge(turned, a * UNITS + (u + 1))
                dve.tensor_copy(probs_t[:, :, :], turn_ps[:, :].rearrange("p (b s) -> p b s", b=BU)).then_inc(turn_copied, 1)

            def rest_at(a, u):
                dve.wait_ge(at_hi_done, a * UNITS + (u + 1))
                half = slice((u % 2) * HALF, (u % 2 + 1) * HALF)
                dve.tensor_tensor(at_lo[:, u // 2, half], pv_ps[:, :], at_hi[:, u // 2, half].bitcast(F32),
                                  ALU.subtract).then_inc(at_split, 1)

            def add_out(a, b):
                dve.wait_ge(out_done, a * B + (b + 1))
                dve.tensor_tensor(acc[:, b, :], proj_ps[b % BANKS][:, :], acc[:, b, :], ALU.add).then_inc(acc_done, 1)

            def iteration(a):
                add_bias(a, 0)
                add_bias(a, 1)
                normalise(a, 0)
                normalise(a, 1)
                copy_turned(a, 0)
                add_bias(a, 2)
                rest_at(a, 0)
                copy_turned(a, 1)
                add_bias(a, 3)
                normalise(a, 2)
                rest_at(a, 1)
                normalise(a, 3)
                copy_turned(a, 2)
                rest_at(a, 2)
                copy_turned(a, 3)
                rest_at(a, 3)
                for b in range(B):
                    add_out(a, b)

            with dve.Fori(0, NPH) as a:
                iteration(a)

            dve.wait_ge(tanh_done, 1)

            def second_norm(i):
                if i % 2 == 0:
                    dve.wait_ge(x2_in, 16 * B)
                dve.wait_ge(acc_done, B * (NPH + 1))
                ordered(dve.scalar_tensor_tensor(out=acc[:, i, :], in0=acc[:, i, :], scalar=tanh_g[:, 0:1], in1=x_again[i],
                                                 op0=ALU.mult, op1=ALU.add))
                ordered(dve.bn_stats(stats[:, i, :], acc[:, i, :]))
                ordered(dve.bn_aggr(mean_var[:, i, :], stats[:, i, :]))
                dve.tensor_scalar(var_e[:, i:i + 1], mean_var[:, i, 1:2], EPS, None, ALU.add).then_inc(var_done, 1)
                refine(3 + i, i, i + 1)
                if i >= 2:
                    dve.wait_ge(xf_turned, i - 1)
                dve.tensor_scalar(xf(i), acc[:, i, :], mean_var[:, i, 0:1], rstd[:, i:i + 1],
                                  ALU.subtract, ALU.mult).then_inc(xf_done, 1)

            def gate(i):
                s = i % 2
                lg = (turn_ps, pv_ps)[s]
                dve.wait_ge(logits_done, i + 1)
                ordered(dve.max(top_v[:, s, :], lg[:, ER:ER + E]))
                dve.tensor_tensor(gap[:, i:i + 1], top_v[:, s, 1:2], top_v[:, s, 0:1], ALU.subtract).then_inc(gap_done, 1)
                ordered(dve.max_index(top_i[:, s, :], top_v[:, s, :], lg[:, ER:ER + E]))
                ordered(dve.tensor_copy(top_f[:, s, :], top_i[:, s, :]))
                dve.wait_ge(e_gap_done, i + 1)
                ordered(dve.tensor_scalar(gate1[:, i:i + 1], e_gap[:, i:i + 1], 1.0, 1.0 / SCALING, ALU.add, ALU.mult))
                ordered(dve.reciprocal(gate1[:, i:i + 1], gate1[:, i:i + 1]))
                ordered(dve.tensor_tensor(gate2[:, i:i + 1], gate1[:, i:i + 1], e_gap[:, i:i + 1], ALU.mult))
                dve.tensor_scalar(pick1[:, s, :], expert_id[:, :], top_f[:, s, 0:1], gate1[:, i:i + 1], ALU.is_equal, ALU.mult)
                ordered(dve.tensor_scalar(pick2[:, s, :], expert_id[:, :], top_f[:, s, 1:2], gate2[:, i:i + 1],
                                          ALU.is_equal, ALU.mult))
                ordered(dve.tensor_tensor(pick1[:, s, :], pick1[:, s, :], pick2[:, s, :], ALU.add))
                if i >= 2:
                    dve.wait_ge(hg_turned, i - 1)
                dve.tensor_tensor(hg[:, s, :].rearrange("p (e r) -> p e r", r=R), lg[:, 0:ER].rearrange("p (e r) -> p e r", r=R),
                                  pick1[:, s, :].unsqueeze(2).to_broadcast([P, E, R]), ALU.mult).then_inc(hg_done, 1)

            def rest_hg(i):
                dve.wait_ge(hg_hi_done, i + 1)
                dve.tensor_tensor(hgt_lo[:, i % 2, :, :], proj_ps[2 + i % 2][0:ERH, 0:2 * P].rearrange("p (e s) -> p e s", e=2),
                                  hgt_hi[:, i % 2, :, :].bitcast(F32), ALU.subtract).then_inc(hg_lo_done, 1)

            def finish(i):
                dve.wait_ge(ffn_done, i + 1)
                if i >= 2:
                    dve.wait_ge(stored[i % 2], 16 * (i // 2))
                dve.scalar_tensor_tensor(out=result[:, i % 2, :], in0=proj_ps[i % 2][:, :], scalar=tanh_g[:, 1:2],
                                         in1=acc[:, i, :], op0=ALU.mult, op1=ALU.add).then_inc(final_done, 1)

            def xf(i):
                return probs[:, i % 2, :, :].rearrange("p b s -> p (b s)")

            dve.wait_ge(ids_done, 1)
            second_norm(0)
            rest_xt(0, xf_hi_done, xf_lo_done)
            second_norm(1)
            for i in range(B):
                gate(i)
                if i + 1 < B:
                    rest_xt(i + 1, xf_hi_done, xf_lo_done)
                rest_hg(i)
                if i + 2 < B:
                    second_norm(i + 2)
                if i >= 1:
                    finish(i - 1)
            finish(B - 1)

        @block.tensor
        def _(pe):
            def split_product(o, lhs, rhs, terms, done=None):
                for n in range(terms):
                    for m, (l, r) in enumerate(((0, 0), (1, 0), (0, 1))):
                        mm = pe.matmul(o, lhs(l, n), rhs(r, n), start=(n == 0 and m == 0), stop=(n == terms - 1 and m == 2))
                return mm

            w2, xt2, ct2, at2 = (w_hi, w_lo), (xt_hi, xt_lo), (ct_hi, ct_lo), (at_hi, at_lo)

            def q_or_k(m, i):
                u, k, act2 = m // 2, (WQ, WK)[m % 2], (xt2, ct2)[m % 2]
                j, half = u // 2, slice((u % 2) * HALF, (u % 2 + 1) * HALF)
                mm = split_product(proj_ps[i][:, :], lambda s, c: w2[s][:, k, c * HP * DH + j * DH:c * HP * DH + (j + 1) * DH],
                                   lambda s, c: act2[s][:, c, half], C)
                mm.then_inc(proj_done, 1)
                return mm

            def v_pair(m, i):
                for b in (2 * m, 2 * m + 1):
                    mm = split_product(proj_ps[i][:, (b % 2) * HP * DH:(b % 2 + 1) * HP * DH],
                                       lambda s, c: ct2[s][:, c, b * P:(b + 1) * P],
                                       lambda s, c: w2[s][:, WV, c * HP * DH:(c + 1) * HP * DH], C)
                mm.then_inc(proj_done, 1)
                return mm

            def scores(a, u):
                j, t = u // 2, u % 2
                if u >= 2:
                    pe.wait_ge(biased, a * UNITS + (u - 1))
                for i in range(BU):
                    b = t * BU + i
                    mm = pe.matmul(score_ps[t][:, i * S:(i + 1) * S], qt[:, j, b * S:(b + 1) * S], kt[:, j, b * S:(b + 1) * S],
                                   start=True, stop=True)
                mm.then_inc(scores_done, 1)

            def turn(a, u):
                pe.wait_ge(probs_done, a * UNITS + (u + 1))
                for i in range(BU):
                    mm = pe.transpose(turn_ps[:, i * S:(i + 1) * S], probs[:, u % 2, i, :], ident[:, :])
                mm.then_inc(turned, 1)

            def pv(a, u):
                j, t = u // 2, u % 2
                pe.wait_ge(turn_copied, a * UNITS + (u + 1))
                if u:
                    pe.wait_ge(at_split, a * UNITS + u)
                for i in range(BU):
                    b = t * BU + i
                    mm = pe.matmul(pv_ps[:, i * S:(i + 1) * S], v_sb[:, b, j * DH:(j + 1) * DH], probs_t[:, i, :],
                                   start=True, stop=True)
                mm.then_inc(pv_done, 1)

            def out_proj(p, b, projected):
                if b < BANKS:
                    if projected:
                        pe.wait_ge(proj_copied, p * PROJ + (QK + b + 1))
                    else:
                        pe.wait_ge(acc_done, p * B + (b + 1 + BANKS - B))
                else:
                    pe.wait_ge(acc_done, p * B + (b + 1 - BANKS))
                mm = split_product(proj_ps[b % BANKS][:, :], lambda s, j: at2[s][:, j, b * P:(b + 1) * P],
                                   lambda s, j: w2[s][:, WO, j * D:(j + 1) * D], HP)
                mm.then_inc(out_done, 1)
                return mm

            pe.wait_ge(w_lo_done[WK], 1)
            pe.wait_ge(ctx_lo_done, C)
            for m in range(UNITS):
                mm = q_or_k(2 * m + 1, m)
            pe.wait_ge(ident_done, 1)
            for i in range(B):
                pe.wait_ge(xn_done, i + 1)
                if i >= 2:
                    pe.wait_ge(xt_lo_done, i - 1)
                for c in range(C):
                    mm = pe.transpose(score_ps[i % 2][:, c * P:(c + 1) * P], xn[:, i % 4, c * P:(c + 1) * P], ident[:, :])
                mm.then_inc(xt_turned, 1)
            pe.wait_ge(w_lo_done[WV], 1)
            for m in range(VC):
                pe.wait_ge(proj_copied, m + 1)
                v_pair(m, m)
            pe.wait_ge(w_lo_done[WQ], 1)
            pe.wait_ge(xt_lo_done, B)
            for m in range(UNITS):
                pe.wait_ge(proj_copied, UNITS + m + 1)
                q_or_k(2 * m, m)

            def iteration(p, project):
                a = p - 1

                def chunk(n):
                    if not project:
                        return
                    if n < BANKS:
                        pe.wait_ge(acc_done, (p - 1) * B + (B - BANKS + n + 1))
                    else:
                        pe.wait_ge(proj_copied, p * PROJ + (n - BANKS + 1))
                    if n == 0:
                        pe.wait_ge(w_lo_done[WQ], p + 1)
                    if n == 1:
                        pe.wait_ge(w_lo_done[WK], p + 1)
                    if n == QK:
                        pe.wait_ge(w_lo_done[WV], p + 1)
                    return q_or_k(n, n % BANKS) if n < QK else v_pair(n - QK, n % BANKS)

                pe.wait_ge(proj_copied, p * PROJ)
                scores(a, 0)
                scores(a, 1)
                for n in (0, 1, 2):
                    chunk(n)
                turn(a, 0)
                scores(a, 2)
                chunk(3)
                pv(a, 0)
                turn(a, 1)
                scores(a, 3)
                chunk(4)
                pv(a, 1)
                chunk(5)
                turn(a, 2)
                chunk(6)
                pv(a, 2)
                turn(a, 3)
                chunk(7)
                pv(a, 3)
                for n in range(QK, PROJ):
                    chunk(n)
                pe.wait_ge(w_lo_done[WO], p)
                pe.wait_ge(at_split, p * UNITS)
                for b in range(B):
                    out_proj(p, b, project)

            with pe.Fori(1, NPH) as p:
                iteration(p, True)
            iteration(NPH, False)

            def turn_xf(i):
                pe.wait_ge(xf_done, i + 1)
                if i >= 2:
                    pe.wait_ge(xf_lo_done, i - 1)
                for c in range(C):
                    mm = pe.transpose(score_ps[i % 2][:, c * P:(c + 1) * P],
                                      probs[:, i % 2, c, :], ident[:, :])
                mm.then_inc(xf_turned, 1)

            def rows(i):
                return lambda s, c: xt2[s][:, c, i * P:(i + 1) * P]

            def logits(i):
                pe.wait_ge(xf_lo_done, i + 1)
                if i >= 2:
                    pe.wait_ge(hg_done, i - 1)
                split_product((turn_ps, pv_ps)[i % 2][:, 0:LG], rows(i), lambda s, c: lg_w[s][:, c, :], C).then_inc(logits_done, 1)

            def base(i):
                if i >= 2:
                    pe.wait_ge(final_done, i - 1)
                else:
                    pe.wait_ge(acc_done, B * (NPH + 1))
                o = proj_ps[i % 2][:, :]
                for c in range(C):
                    for m, (l, r) in enumerate(((0, 0), (1, 0), (0, 1))):
                        pe.matmul(o, rows(i)(l, c), base_w[r][:, c, :], start=(c == 0 and m == 0), stop=False)

            def turn_hg(i):
                pe.wait_ge(hg_done, i + 1)
                if i >= 2:
                    pe.wait_ge(hg_lo_done, i - 1)
                for e in range(2):
                    mm = pe.transpose(proj_ps[2 + i % 2][0:ERH, e * P:(e + 1) * P], hg[:, i % 2, e * ERH:(e + 1) * ERH], ident[:, :])
                mm.then_inc(hg_turned, 1)

            def lora(i):
                pe.wait_ge(hg_lo_done, i + 1)
                pe.wait_ge(w_lo_done[WO], NPH + 1)
                o = proj_ps[i % 2][:, :]
                for e in range(2):
                    for m, (l, r) in enumerate(((0, 0), (1, 0), (0, 1))):
                        mm = pe.matmul(o, (hgt_hi, hgt_lo)[l][:, i % 2, e, :], lb_w[r][:, e, :], start=False, stop=(e == 1 and m == 2))
                mm.then_inc(ffn_done, 1)

            for k in (WQ, WK, WV):
                pe.wait_ge(w_lo_done[k], NPH + 1)
            turn_xf(0)
            for i in range(B):
                logits(i)
                if i + 1 < B:
                    turn_xf(i + 1)
                if i >= 1:
                    lora(i - 1)
                base(i)
                turn_hg(i)
            lora(B - 1)


def kernel(**inputs):
    import numpy as np
    import concourse.bacc as bacc
    from concourse.bass_utils import run_bass_kernel_spmd

    a = {k: np.asarray(v) for k, v in inputs.items()}

    def by_phase(w):
        return w.reshape(NPH, HP, DH, C, P).transpose(0, 4, 3, 1, 2).reshape(NPH, P, WN)

    weights = np.zeros((NPH + 1, 4, P, WN), np.float32)
    for k, name in ((WQ, "w_q"), (WK, "w_k"), (WV, "w_v")):
        weights[:NPH, k] = by_phase(a["L0_xattn_" + name])
    weights[:NPH, WO] = a["L0_xattn_w_out"].reshape(D, NPH, HP, DH).transpose(1, 3, 2, 0).reshape(NPH, P, HP * D)
    base = a["L0_ffn_base_W"].T.reshape(C, P, D).transpose(1, 0, 2).reshape(P, 2, WN)
    weights[NPH, 0:2] = base.transpose(1, 0, 2)
    lg = np.zeros((D, LG), np.float32)
    lg[:, :ER] = a["L0_ffn_lora_A"].reshape(ER, D).T
    lg[:, ER:ER + E] = a["L0_ffn_gate_W"].T
    weights[NPH, 2] = lg.reshape(C, P, LG).transpose(1, 0, 2).reshape(P, WN)
    lb = a["L0_ffn_lora_B"].transpose(0, 2, 1).reshape(2, ERH, D)
    weights[NPH, 3, :ERH] = lb.transpose(1, 0, 2).reshape(ERH, WN)

    arrays = {
        "x": a["x"],
        "ctx_t": np.ascontiguousarray(a["ctx_4096"].reshape(T, D).T).reshape(C, P, T),
        "weights": weights,
        "bias": np.ascontiguousarray(a["L0_xattn_position_bias"].reshape(NPH, HP, S, S).transpose(0, 2, 1, 3)),
        "mask": np.ascontiguousarray(a["mask_BxSxS2_bk0"]),
        "g_x": a["g_xattn"], "g_f": a["g_ffn"], "ln_w": a["L0_xattn_ln_weight"],
    }
    nc = bacc.Bacc("TRN2", target_bir_lowering=False, num_devices=1)
    args = [nc.dram_tensor("in_" + n, v.shape, mybir.dt.from_np(v.dtype), kind="ExternalInput").ap() for n, v in arrays.items()]
    out = nc.dram_tensor("out", (B, S, D), F32, kind="ExternalOutput").ap()
    build(nc, *args, out)
    r = run_bass_kernel_spmd(nc, [{"in_" + n: v for n, v in arrays.items()}], core_ids=[0])
    return r.results[0]["out"]
```

```python
from contextlib import ExitStack

import concourse.bass as bass
from concourse import mybir

F32 = mybir.dt.float32
F32R = mybir.dt.float32r
U8 = mybir.dt.uint8
U32 = mybir.dt.uint32
ALU = mybir.AluOpType
ACT = mybir.ActivationFunctionType
AX = mybir.AxisListType

P = 128
B, S, D = 8, 128, 512
H, DH = 32, 128
E, R, TOP = 28, 8, 2
SCALING = 16 / R
EPS = 1e-5
NEG = -1e30
T = B * S
C = D // P
HP = 2
NPH = H // HP
HALF = T // 2
UNITS = HP * 2
BU = B // 2
QK = 2 * UNITS
VC = B // 2
PROJ = QK + VC
BANKS = 4
WQ, WK, WV, WO = range(4)
WN = C * HP * DH
ER = E * R
ERH = ER // 2
G = B // 2
LG = 256


def build(nc, x, ctx_t, weights, bias, mask, g_x, g_f, ln_w, out):
    ctx = ExitStack()
    with ctx:
        def sb(name, shape, dt=F32):
            return ctx.enter_context(nc.sbuf_tensor(name, shape, dt))

        def sem(name):
            return ctx.enter_context(nc.semaphore(name))

        def bank(name):
            return ctx.enter_context(nc.psum_tensor(name, [P, 512], F32))

        xt_hi, xt_lo = sb("xt_hi", [P, C, T], F32R), sb("xt_lo", [P, C, T], F32R)
        ct_hi, ct_lo = sb("ct_hi", [P, C, T], F32R), sb("ct_lo", [P, C, T], F32R)
        w_hi, w_lo = sb("w_hi", [P, 4, WN], F32R), sb("w_lo", [P, 4, WN], F32R)
        w_raw = sb("w_raw", [P, 4, WN])
        qt, kt = sb("qt", [P, HP, T]), sb("kt", [P, HP, T])
        v_sb = sb("v_sb", [P, B, HP * DH])
        at_hi, at_lo = sb("at_hi", [P, HP, T], F32R), sb("at_lo", [P, HP, T], F32R)
        acc = sb("acc", [P, B, D])
        bias_sb = sb("bias_sb", [P, HP, S])
        comb = sb("comb", [P, HP, B, S])
        mask_u8 = sb("mask_u8", [P, B, S], U8)
        mask_add = sb("mask_add", [P, B, S])
        row_any = sb("row_any", [P, B])
        probs = sb("probs", [P, UNITS, BU, S])
        probs_t = sb("probs_t", [P, BU, S])
        neg_max, row_sum, row_scale = (sb(n, [P, UNITS, BU]) for n in ("neg_max", "row_sum", "row_scale"))
        ident = sb("ident", [P, P])
        lnw = sb("lnw", [P, D])
        gates = sb("gates", [P, 2])
        tanh_g = sb("tanh_g", [P, 2])
        stats = sb("stats", [P, B, 6])
        mean_var = sb("mean_var", [P, B, 2])
        pow_half = sb("pow_half", [P, B])
        var_e, rstd, newton = sb("var_e", [P, B]), sb("rstd", [P, B]), sb("newton", [P, B])
        rms = sb("rms", [P, B])
        shift = sb("shift", [P, B])
        warm = sb("warm", [P, 1])
        expert_id = sb("expert_id", [P, E])
        top_v, top_i, top_f = sb("top_v", [P, B, 8]), sb("top_i", [P, B, 8], U32), sb("top_f", [P, B, 8])
        gap, e_gap, gate1, gate2 = (sb(n, [P, B]) for n in ("gap", "e_gap", "gate1", "gate2"))
        pick1, pick2 = sb("pick1", [P, G, E]), sb("pick2", [P, G, E])
        hg = sb("hg", [P, G, ER])
        hgt_hi, hgt_lo = sb("hgt_hi", [ERH, 2, 2, P], F32R), sb("hgt_lo", [ERH, 2, 2, P], F32R)

        score_ps = [bank(f"score_ps{i}") for i in range(2)]
        turn_ps, pv_ps = bank("turn_ps"), bank("pv_ps")
        proj_ps = [bank(f"proj_ps{i}") for i in range(BANKS)]

        ctx_raw = [t[:, i, :] for t in (qt, kt) for i in range(HP)]
        xn = comb[:, :, :, :].rearrange("p h (a b) s -> p (h a) (b s)", b=D // S)
        xf = v_sb[:, :, :].rearrange("p (i n) d -> p i (n d)", n=2)
        result = probs[:, :, :, :].rearrange("p n b s -> p n (b s)")
        x_again = [w_raw[:, i // 2, (i % 2) * D:(i % 2 + 1) * D] for i in range(6)] + [qt[:, 0, i * D:(i + 1) * D] for i in range(2)]
        base_w = [w[:, 0:2, :].rearrange("p a (c n) -> p (a c) n", n=D) for w in (w_hi, w_lo)]
        lg_w = [w[:, 2, :].rearrange("p (c n) -> p c n", n=LG) for w in (w_hi, w_lo)]
        lb_w = [w[0:ERH, 3, :].rearrange("p (e n) -> p e n", n=D) for w in (w_hi, w_lo)]

        def lg_ps(i):
            return (turn_ps, pv_ps)[i % G // 2][:, (i % 2) * LG:(i % 2 + 1) * LG]

        hgt_ps = proj_ps[3][0:ERH, :].rearrange("p (i e s) -> p i e s", i=2, e=2)

        x_in = [sem(f"x_in{i}") for i in range(4)]
        ctx_in = [sem(f"ctx_in{i}") for i in range(C)]
        w_in = [sem(f"w_in{k}") for k in range(4)]
        bias_in, mask_in, small_in = sem("bias_in"), sem("mask_in"), sem("small_in")
        x2_in = [sem(f"x2_in{i}") for i in range(B)]
        stored = [sem(f"stored{i}") for i in range(UNITS)]
        w_hi_done = [sem(f"w_hi_done{k}") for k in range(4)]
        w_lo_done = [sem(f"w_lo_done{k}") for k in range(4)]
        ctx_hi_done, ctx_lo_done = sem("ctx_hi_done"), sem("ctx_lo_done")
        ident_zero, ident_done, pow_const, ids_done = sem("ident_zero"), sem("ident_done"), sem("pow_const"), sem("ids_done")
        dve_step = sem("dve_step")
        var_done, rstd0_done = sem("var_done"), sem("rstd0_done")
        xn_done, xt_turned = sem("xn_done"), sem("xt_turned")
        xt_hi_done, xt_lo_done = sem("xt_hi_done"), sem("xt_lo_done")
        acc_done = sem("acc_done")
        mask_done, comb_done, tanh_done = sem("mask_done"), sem("comb_done"), sem("tanh_done")
        proj_done, proj_copied = sem("proj_done"), sem("proj_copied")
        scores_done, biased, max_done = sem("scores_done"), sem("biased"), sem("max_done")
        exp_done, scaled, probs_done = sem("exp_done"), sem("scaled"), sem("probs_done")
        turned, turn_copied = sem("turned"), sem("turn_copied")
        pv_done, at_hi_done, at_split = sem("pv_done"), sem("at_hi_done"), sem("at_split")
        out_done = sem("out_done")
        resid_done, shift_done = sem("resid_done"), sem("shift_done")
        xf_done, xf_turned, xf_hi_done, xf_lo_done = sem("xf_done"), sem("xf_turned"), sem("xf_hi_done"), sem("xf_lo_done")
        logits_done, gap_done, e_gap_done = sem("logits_done"), sem("gap_done"), sem("e_gap_done")
        hg_done, hg_turned, hg_hi_done, hg_lo_done = sem("hg_done"), sem("hg_turned"), sem("hg_hi_done"), sem("hg_lo_done")
        ffn_done, final_done = sem("ffn_done"), sem("final_done")

        block = ctx.enter_context(nc.Block())

        @block.sync
        def _(sp):
            def load_w(k, p):
                sp.dma_start(w_raw[:, k, :], weights[p, k] if isinstance(p, int)
                             else weights[bass.ds(p, 1), k].rearrange("a p n -> p (a n)")).then_inc(w_in[k], 16)

            def load_x(i):
                sp.dma_start(acc[:, 2 * i:2 * i + 2, :], x[2 * i:2 * i + 2].rearrange("b s d -> s b d")).then_inc(x_in[i], 16)

            load_w(WK, 0)
            for c in range(C):
                sp.dma_start(ctx_raw[c], ctx_t[c]).then_inc(ctx_in[c], 16)
            load_x(0)
            load_x(1)
            load_w(WV, 0)
            load_x(2)
            load_x(3)
            load_w(WQ, 0)
            sp.dma_start(mask_u8[:, :, :], mask.rearrange("b q k -> q b k")).then_inc(mask_in, 16)
            sp.dma_start(bias_sb[:, :, :], bias[0]).then_inc(bias_in, 16)
            load_w(WO, 0)

            def refill(p):
                for k in (WQ, WK, WV):
                    sp.wait_ge(w_lo_done[k], p + 1)
                    load_w(k, p + 1)

            def refill_out(p):
                sp.wait_ge(w_lo_done[WO], p + 1)
                load_w(WO, p + 1)

            with sp.Fori(0, NPH - 1) as p:
                refill(p)
                sp.wait_ge(comb_done, p * HP + HP)
                sp.dma_start(bias_sb[:, :, :], bias[bass.ds(p + 1, 1)].rearrange("a q h k -> q (a h) k")).then_inc(bias_in, 16)
                refill_out(p)
            refill(NPH - 1)
            refill_out(NPH - 1)
            for i in range(6):
                sp.wait_ge(w_lo_done[i // 2], NPH + 1)
                sp.dma_start(x_again[i], x[i]).then_inc(x2_in[i], 16)
            sp.wait_ge(scores_done, UNITS * NPH)
            for i in range(6, B):
                sp.dma_start(x_again[i], x[i]).then_inc(x2_in[i], 16)
            for i in range(B):
                sp.wait_ge(final_done, i + 1)
                sp.dma_start(out[i], result[:, i % UNITS, :]).then_inc(stored[i % UNITS], 16)
            for s in stored:
                sp.wait_ge(s, 16 * (B // UNITS))

        @block.gpsimd
        def _(pool):
            pool.memset(ident[:, :], 0.0).then_inc(ident_zero, 1)
            pool.wait_ge(ident_zero, 1)
            pool.affine_select(out=ident[:, :], in_=ident[:, :], compare_op=ALU.not_equal, fill=1.0, base=0,
                               pattern=[[-1, P]], channel_multiplier=1).then_inc(ident_done, 1)
            pool.memset(pow_half[:, :], -0.5).then_inc(pow_const, 1)
            pool.iota(expert_id[:, :], pattern=[[1, E]], base=0, channel_multiplier=0,
                      allow_small_or_imprecise_dtypes=True).then_inc(ids_done, 1)

            def rest(k, p):
                pool.wait_ge(w_hi_done[k], p + 1)
                pool.tensor_tensor(w_lo[:, k, :], w_raw[:, k, :], w_hi[:, k, :].bitcast(F32),
                                   ALU.subtract).then_inc(w_lo_done[k], 1)

            def add_mask(p, first):
                pool.wait_ge(bias_in, (p + 1) * 16)
                for j in range(HP):
                    if not first:
                        pool.wait_ge(biased, (p - 1) * UNITS + (HP + j + 1))
                    pool.tensor_tensor(comb[:, j, :, :], mask_add[:, :, :],
                                       bias_sb[:, j:j + 1, :].to_broadcast([P, B, S]), ALU.add).then_inc(comb_done, 1)

            def inverse_root(n, v, r):
                pool.wait_ge(var_done, n)
                pool.tensor_tensor(r, v, pow_half[:, 0:G], ALU.pow).then_inc(rstd0_done, 1)

            pool.wait_ge(pow_const, 1)
            rest(WV, 0)
            for g in range(2):
                at = slice(g * G, (g + 1) * G)
                inverse_root(2 * g + 1, var_e[:, at], rstd[:, at])
                inverse_root(2 * g + 2, var_e[:, at], rms[:, at])
            rest(WQ, 0)
            pool.wait_ge(mask_done, 1)
            pool.wait_ge(xt_turned, B)
            add_mask(0, True)
            for k in (WQ, WK, WV):
                rest(k, 1)
            rest(WO, 0)
            with pool.Fori(1, NPH) as p:
                add_mask(p, False)
                for k in (WQ, WK, WV):
                    rest(k, p + 1)
                rest(WO, p)
            for g in range(2):
                at = slice(g * G, (g + 1) * G)
                inverse_root(5 + g, var_e[:, at], rstd[:, at])
                if g == 0:
                    rest(WO, NPH)

        @block.scalar
        def _(act):
            act.dma_start(lnw[:, :], ln_w.rearrange("(a n) -> a n", a=1).to_broadcast([P, D])).then_inc(small_in, 16)
            act.dma_start(gates[:, 0:1], g_x.rearrange("(a n) -> a n", a=1).to_broadcast([P, 1])).then_inc(small_in, 16)
            act.dma_start(gates[:, 1:2], g_f.rearrange("(a n) -> a n", a=1).to_broadcast([P, 1])).then_inc(small_in, 16)

            def lead(k, p):
                act.wait_ge(w_in[k], (p + 1) * 16)
                act.activation(w_hi[:, k, :], w_raw[:, k, :], ACT.Copy).then_inc(w_hi_done[k], 1)

            def copy_proj(p, n, i, dst):
                act.wait_ge(proj_done, p * PROJ + (n + 1))
                act.activation(dst, proj_ps[i][:, :], ACT.Copy).then_inc(proj_copied, 1)

            def q_or_k(m):
                u, t = m // 2, (qt, kt)[m % 2]
                return t[:, u % HP, (u // HP) * HALF:(u // HP + 1) * HALF]

            def v_dst(m):
                return v_sb[:, 2 * m:2 * m + 2, :].rearrange("p b d -> p (b d)")

            def exps(a, u):
                act.wait_ge(max_done, a * UNITS + (u + 1))
                for i in range(BU):
                    e = act.activation(probs[:, u, i, :], probs[:, u, i, :], ACT.Exp,
                                       bias=neg_max[:, u, i:i + 1], accum_out=row_sum[:, u, i:i + 1])
                e.then_inc(exp_done, 1)

            def lead_at(a, u):
                act.wait_ge(pv_done, a * UNITS + (u + 1))
                act.activation(at_hi[:, u % HP, (u // HP) * HALF:(u // HP + 1) * HALF], pv_ps[:, :],
                               ACT.Copy).then_inc(at_hi_done, 1)

            def lead_xt(i):
                act.wait_ge(xt_turned, i + 1)
                act.activation(xt_hi[:, :, i * P:(i + 1) * P], score_ps[i % 2][:, :].rearrange("p (c s) -> p c s", c=C),
                               ACT.Copy).then_inc(xt_hi_done, 1)

            act.wait_ge(pow_const, 1)
            act.activation(warm[:, :], pow_half[:, 0:1], ACT.Exp)
            lead(WK, 0)
            for c in range(C):
                act.wait_ge(ctx_in[c], 16)
                act.activation(ct_hi[:, c, :], ctx_raw[c], ACT.Copy).then_inc(ctx_hi_done, 1)
            lead(WV, 0)
            for m in range(UNITS):
                copy_proj(0, m, m % BANKS, q_or_k(2 * m + 1))
            lead(WQ, 0)
            act.wait_ge(small_in, 48)
            act.activation(tanh_g[:, :], gates[:, :], ACT.Tanh).then_inc(tanh_done, 1)
            for g in range(2):
                for m in range(g * VC // 2, (g + 1) * VC // 2):
                    copy_proj(0, UNITS + m, m % BANKS, v_dst(m))
                for i in range(g * G, (g + 1) * G):
                    lead_xt(i)
            for m in range(UNITS):
                copy_proj(0, UNITS + VC + m, m % BANKS, q_or_k(2 * m))
            for k in (WQ, WK, WV):
                lead(k, 1)
            lead(WO, 0)

            def iteration(p):
                a = p - 1

                def chunk(n):
                    copy_proj(p, n, n % BANKS, q_or_k(n) if n < QK else v_dst(n - QK))

                exps(a, 0)
                chunk(0)
                exps(a, 1)
                chunk(1)
                chunk(2)
                exps(a, 2)
                lead_at(a, 0)
                chunk(3)
                exps(a, 3)
                lead_at(a, 1)
                for n in (4, 5, 6):
                    chunk(n)
                lead_at(a, 2)
                chunk(7)
                lead_at(a, 3)
                for n in range(QK, PROJ):
                    chunk(n)
                for k in (WQ, WK, WV):
                    lead(k, p + 1)
                act.wait_ge(out_done, p * B)
                lead(WO, p)

            with act.Fori(1, NPH) as p:
                iteration(p)
            exps(NPH - 1, 0)
            exps(NPH - 1, 1)
            exps(NPH - 1, 2)
            lead_at(NPH - 1, 0)
            exps(NPH - 1, 3)
            for u in (1, 2, 3):
                lead_at(NPH - 1, u)

            def norm_xf(i):
                act.wait_ge(shift_done, i // G + 1)
                if i >= G:
                    act.wait_ge(xf_turned, i - G + 1)
                act.activation(xf[:, i % G, :], acc[:, i, :], ACT.Identity, bias=shift[:, i:i + 1],
                               scale=rstd[:, i:i + 1]).then_inc(xf_done, 1)

            def lead_xf(i):
                act.wait_ge(xf_turned, i + 1)
                act.activation(xt_hi[:, :, i * P:(i + 1) * P], score_ps[i % 2][:, :].rearrange("p (c s) -> p c s", c=C),
                               ACT.Copy).then_inc(xf_hi_done, 1)

            def exp_gap(g):
                act.wait_ge(gap_done, g + 1)
                act.activation(e_gap[:, g * G:(g + 1) * G], gap[:, g * G:(g + 1) * G], ACT.Exp).then_inc(e_gap_done, 1)

            def lead_hg(n):
                act.wait_ge(hg_turned, n + 1)
                if n:
                    act.wait_ge(ffn_done, 2 * n)
                act.activation(hgt_hi[:, :, :, :], hgt_ps, ACT.Copy).then_inc(hg_hi_done, 1)

            for i in range(G):
                norm_xf(i)
            act.wait_ge(out_done, NPH * B)
            lead(WO, NPH)
            for i in range(G):
                lead_xf(i)
            for i in range(G, B):
                norm_xf(i)
            for i in range(G, B):
                lead_xf(i)
            exp_gap(0)
            lead_hg(0)
            exp_gap(1)
            for n in range(1, B // 2):
                lead_hg(n)

        @block.vector
        def _(dve):
            steps = [0]

            def ordered(ins):
                steps[0] += 1
                ins.then_inc(dve_step, 1)
                dve.wait_ge(dve_step, steps[0])

            def refine(n, r, v, t):
                dve.wait_ge(rstd0_done, n)
                ordered(dve.tensor_tensor(t, r, r, ALU.mult))
                ordered(dve.scalar_tensor_tensor(out=t, in0=t, scalar=-0.5, in1=v, op0=ALU.mult, op1=ALU.mult))
                ordered(dve.scalar_tensor_tensor(out=r, in0=t, scalar=1.5, in1=r, op0=ALU.add, op1=ALU.mult))

            def variances(i0):
                for i in range(i0, i0 + G):
                    ordered(dve.bn_aggr(mean_var[:, i, :], stats[:, i, :]))
                dve.tensor_scalar(var_e[:, i0:i0 + G], mean_var[:, i0:i0 + G, 1], EPS, None, ALU.add).then_inc(var_done, 1)

            def rest_ctx(c):
                dve.wait_ge(ctx_hi_done, c + 1)
                dve.tensor_tensor(ct_lo[:, c, :], ctx_raw[c], ct_hi[:, c, :].bitcast(F32), ALU.subtract).then_inc(ctx_lo_done, 1)

            dve.wait_ge(w_hi_done[WK], 1)
            dve.tensor_tensor(w_lo[:, WK, :], w_raw[:, WK, :], w_hi[:, WK, :].bitcast(F32), ALU.subtract).then_inc(w_lo_done[WK], 1)
            for c in range(C):
                rest_ctx(c)

            def rest_xt(i, hi_done, lo_done):
                dve.wait_ge(hi_done, i + 1)
                dve.tensor_tensor(xt_lo[:, :, i * P:(i + 1) * P], score_ps[i % 2][:, :].rearrange("p (c s) -> p c s", c=C),
                                  xt_hi[:, :, i * P:(i + 1) * P].bitcast(F32), ALU.subtract).then_inc(lo_done, 1)

            for g in range(2):
                at = slice(g * G, (g + 1) * G)
                tiles = range(g * G, (g + 1) * G)
                for i in tiles:
                    if i % 2 == 0:
                        dve.wait_ge(x_in[i // 2], 16)
                    st = dve.bn_stats(stats[:, i, :], acc[:, i, :])
                ordered(st)
                variances(g * G)
                refine(2 * g + 1, rstd[:, at], var_e[:, at], newton[:, at])
                ordered(dve.tensor_tensor(newton[:, at], rstd[:, at], rstd[:, at], ALU.mult))
                ordered(dve.tensor_tensor(newton[:, at], newton[:, at], mean_var[:, at, 1], ALU.mult))
                dve.tensor_scalar(var_e[:, at], newton[:, at], EPS, None, ALU.add).then_inc(var_done, 1)
                refine(2 * g + 2, rms[:, at], var_e[:, at], newton[:, at])
                for i in tiles:
                    dve.tensor_scalar(acc[:, i, :], acc[:, i, :], mean_var[:, i, 0:1], rstd[:, i:i + 1],
                                      ALU.subtract, ALU.mult).then_inc(acc_done, 1)
                if g == 0:
                    dve.wait_ge(small_in, 48)
                for i in tiles:
                    dve.wait_ge(acc_done, i + 1)
                    if g:
                        dve.wait_ge(xt_turned, i - G + 1)
                    dve.scalar_tensor_tensor(out=xn[:, i % G, :], in0=acc[:, i, :], scalar=rms[:, i:i + 1], in1=lnw[:, :],
                                             op0=ALU.mult, op1=ALU.mult).then_inc(xn_done, 1)
                for i in tiles:
                    rest_xt(i, xt_hi_done, xt_lo_done)
            dve.wait_ge(mask_in, 16)
            dve.tensor_scalar(mask_add[:, :, :], mask_u8[:, :, :], 1.0, -NEG, ALU.subtract, ALU.mult).then_inc(mask_done, 1)
            ordered(dve.tensor_reduce(row_any[:, :], mask_u8[:, :, :], AX.X, ALU.max))

            def add_bias(a, u):
                j, t = u % HP, u // HP
                dve.wait_ge(scores_done, a * UNITS + (u + 1))
                dve.wait_ge(comb_done, a * HP + (j + 1))
                dve.tensor_tensor(probs[:, u, :, :], score_ps[u % 2][:, :].rearrange("p (b s) -> p b s", b=BU),
                                  comb[:, j, t * BU:(t + 1) * BU, :], ALU.add).then_inc(biased, 1)
                dve.wait_ge(biased, a * UNITS + (u + 1))
                dve.tensor_reduce(neg_max[:, u, :], probs[:, u, :, :], AX.X, ALU.max, negate=True).then_inc(max_done, 1)

            def normalise(a, u):
                t = u // HP
                dve.wait_ge(exp_done, a * UNITS + (u + 1))
                dve.reciprocal(row_scale[:, u, :], row_sum[:, u, :]).then_inc(scaled, 1)
                dve.wait_ge(scaled, a * (2 * UNITS) + (2 * u + 1))
                dve.tensor_tensor(row_scale[:, u, :], row_scale[:, u, :], row_any[:, t * BU:(t + 1) * BU],
                                  ALU.mult).then_inc(scaled, 1)
                dve.wait_ge(scaled, a * (2 * UNITS) + (2 * u + 2))
                dve.tensor_tensor(probs[:, u, :, :], probs[:, u, :, :],
                                  row_scale[:, u, :].unsqueeze(2).to_broadcast([P, BU, S]), ALU.mult).then_inc(probs_done, 1)

            def copy_turned(a, u):
                dve.wait_ge(turned, a * UNITS + (u + 1))
                dve.tensor_copy(probs_t[:, :, :], turn_ps[:, :].rearrange("p (b s) -> p b s", b=BU)).then_inc(turn_copied, 1)

            def rest_at(a, u):
                dve.wait_ge(at_hi_done, a * UNITS + (u + 1))
                half = slice((u // HP) * HALF, (u // HP + 1) * HALF)
                dve.tensor_tensor(at_lo[:, u % HP, half], pv_ps[:, :], at_hi[:, u % HP, half].bitcast(F32),
                                  ALU.subtract).then_inc(at_split, 1)

            def add_out(a, b):
                dve.wait_ge(out_done, a * B + (b + 1))
                dve.tensor_tensor(acc[:, b, :], proj_ps[b % BANKS][:, :], acc[:, b, :], ALU.add).then_inc(acc_done, 1)

            def iteration(a):
                add_bias(a, 0)
                add_bias(a, 1)
                normalise(a, 0)
                normalise(a, 1)
                copy_turned(a, 0)
                add_bias(a, 2)
                rest_at(a, 0)
                copy_turned(a, 1)
                add_bias(a, 3)
                normalise(a, 2)
                rest_at(a, 1)
                normalise(a, 3)
                copy_turned(a, 2)
                rest_at(a, 2)
                copy_turned(a, 3)
                rest_at(a, 3)
                for b in range(B):
                    add_out(a, b)

            with dve.Fori(0, NPH - 1) as a:
                iteration(a)

            last = NPH - 1
            dve.wait_ge(tanh_done, 1)
            dve.wait_ge(acc_done, B * NPH)

            def residual(i):
                dve.wait_ge(x2_in[i], 16)
                dve.scalar_tensor_tensor(out=acc[:, i, :], in0=acc[:, i, :], scalar=tanh_g[:, 0:1], in1=x_again[i],
                                         op0=ALU.mult, op1=ALU.add).then_inc(resid_done, 1)

            def last_out(i):
                dve.wait_ge(resid_done, i + 1)
                dve.wait_ge(out_done, last * B + i + 1)
                dve.scalar_tensor_tensor(out=acc[:, i, :], in0=proj_ps[i % BANKS][:, :], scalar=tanh_g[:, 0:1],
                                         in1=acc[:, i, :], op0=ALU.mult, op1=ALU.add).then_inc(acc_done, 1)

            def statistics(i):
                dve.wait_ge(acc_done, B * NPH + i + 1)
                return dve.bn_stats(stats[:, i, :], acc[:, i, :])

            def second_norm(g):
                at = slice(g * G, (g + 1) * G)
                refine(5 + g, rstd[:, at], var_e[:, at], newton[:, at])
                dve.scalar_tensor_tensor(out=shift[:, at], in0=mean_var[:, at, 0], scalar=-1.0, in1=rstd[:, at],
                                         op0=ALU.mult, op1=ALU.mult).then_inc(shift_done, 1)

            def best(g):
                for i in range(g * G, (g + 1) * G):
                    dve.wait_ge(logits_done, i // 2 * 2 + 2)
                    m = dve.max(top_v[:, i, :], lg_ps(i)[:, ER:ER + E])
                ordered(m)
                at = slice(g * G, (g + 1) * G)
                dve.tensor_tensor(gap[:, at], top_v[:, at, 1], top_v[:, at, 0], ALU.subtract).then_inc(gap_done, 1)
                for i in range(g * G, (g + 1) * G):
                    m = dve.max_index(top_i[:, i, :], top_v[:, i, :], lg_ps(i)[:, ER:ER + E])
                ordered(m)
                ordered(dve.tensor_copy(top_f[:, at, :], top_i[:, at, :]))

            def gate(g):
                at = slice(g * G, (g + 1) * G)
                dve.wait_ge(e_gap_done, g + 1)
                ordered(dve.tensor_scalar(gate1[:, at], e_gap[:, at], 1.0, 1.0 / SCALING, ALU.add, ALU.mult))
                ordered(dve.reciprocal(gate1[:, at], gate1[:, at]))
                ordered(dve.tensor_tensor(gate2[:, at], gate1[:, at], e_gap[:, at], ALU.mult))
                for i in range(g * G, (g + 1) * G):
                    dve.tensor_scalar(pick1[:, i % G, :], expert_id[:, :], top_f[:, i, 0:1], gate1[:, i:i + 1], ALU.is_equal, ALU.mult)
                    m = dve.tensor_scalar(pick2[:, i % G, :], expert_id[:, :], top_f[:, i, 1:2], gate2[:, i:i + 1],
                                          ALU.is_equal, ALU.mult)
                ordered(m)
                ordered(dve.tensor_tensor(pick1[:, :, :], pick1[:, :, :], pick2[:, :, :], ALU.add))
                for i in range(g * G, (g + 1) * G):
                    if g:
                        dve.wait_ge(hg_turned, (i - G) // 2 + 1)
                    dve.tensor_tensor(hg[:, i % G, :].rearrange("p (e r) -> p e r", r=R),
                                      lg_ps(i)[:, 0:ER].rearrange("p (e r) -> p e r", r=R),
                                      pick1[:, i % G, :].unsqueeze(2).to_broadcast([P, E, R]), ALU.mult).then_inc(hg_done, 1)

            def rest_hg(n):
                dve.wait_ge(hg_hi_done, n + 1)
                dve.tensor_tensor(hgt_lo[:, :, :, :], hgt_ps, hgt_hi[:, :, :, :].bitcast(F32),
                                  ALU.subtract).then_inc(hg_lo_done, 1)

            def finish(i):
                dve.wait_ge(ffn_done, i + 1)
                if i >= UNITS:
                    dve.wait_ge(stored[i % UNITS], 16 * (i // UNITS))
                dve.scalar_tensor_tensor(out=result[:, i % UNITS, :], in0=proj_ps[i % 3][:, :], scalar=tanh_g[:, 1:2],
                                         in1=acc[:, i, :], op0=ALU.mult, op1=ALU.add).then_inc(final_done, 1)

            add_bias(last, 0)
            add_bias(last, 1)
            normalise(last, 0)
            add_bias(last, 2)
            normalise(last, 1)
            copy_turned(last, 0)
            add_bias(last, 3)
            rest_at(last, 0)
            copy_turned(last, 1)
            normalise(last, 2)
            rest_at(last, 1)
            residual(0)
            residual(1)
            normalise(last, 3)
            last_out(0)
            residual(2)
            copy_turned(last, 2)
            last_out(1)
            residual(3)
            rest_at(last, 2)
            copy_turned(last, 3)
            statistics(0)
            last_out(2)
            statistics(1)
            last_out(3)
            rest_at(last, 3)
            statistics(2)
            ordered(statistics(3))
            variances(0)
            for i in range(G, B):
                residual(i)
            second_norm(0)
            for i in range(G, B):
                last_out(i)
                st = statistics(i)
            ordered(st)
            variances(G)
            rest_xt(0, xf_hi_done, xf_lo_done)
            second_norm(1)
            for i in range(1, G):
                rest_xt(i, xf_hi_done, xf_lo_done)
            dve.wait_ge(ids_done, 1)
            best(0)
            for i in range(G, B):
                rest_xt(i, xf_hi_done, xf_lo_done)
            gate(0)
            rest_hg(0)
            best(1)
            finish(0)
            finish(1)
            rest_hg(1)
            gate(1)
            finish(2)
            finish(3)
            for n in (2, 3):
                rest_hg(n)
                finish(2 * n)
                finish(2 * n + 1)

        @block.tensor
        def _(pe):
            def split_product(o, lhs, rhs, terms, each=None):
                for n in range(terms):
                    if each:
                        each(n)
                    for m, (l, r) in enumerate(((0, 0), (1, 0), (0, 1))):
                        mm = pe.matmul(o, lhs(l, n), rhs(r, n), start=(n == 0 and m == 0), stop=(n == terms - 1 and m == 2))
                return mm

            w2, xt2, ct2, at2 = (w_hi, w_lo), (xt_hi, xt_lo), (ct_hi, ct_lo), (at_hi, at_lo)

            def q_or_k(m, i, each=None):
                u, k, act2 = m // 2, (WQ, WK)[m % 2], (xt2, ct2)[m % 2]
                j, half = u % HP, slice((u // HP) * HALF, (u // HP + 1) * HALF)
                mm = split_product(proj_ps[i][:, :], lambda s, c: w2[s][:, k, c * HP * DH + j * DH:c * HP * DH + (j + 1) * DH],
                                   lambda s, c: act2[s][:, c, half], C, each)
                mm.then_inc(proj_done, 1)
                return mm

            def v_pair(m, i):
                for b in (2 * m, 2 * m + 1):
                    mm = split_product(proj_ps[i][:, (b % 2) * HP * DH:(b % 2 + 1) * HP * DH],
                                       lambda s, c: ct2[s][:, c, b * P:(b + 1) * P],
                                       lambda s, c: w2[s][:, WV, c * HP * DH:(c + 1) * HP * DH], C)
                mm.then_inc(proj_done, 1)
                return mm

            def scores(a, u):
                j, t = u % HP, u // HP
                if u >= 2:
                    pe.wait_ge(biased, a * UNITS + (u - 1))
                for i in range(BU):
                    b = t * BU + i
                    mm = pe.matmul(score_ps[u % 2][:, i * S:(i + 1) * S], qt[:, j, b * S:(b + 1) * S], kt[:, j, b * S:(b + 1) * S],
                                   start=True, stop=True)
                mm.then_inc(scores_done, 1)

            def turn(a, u):
                pe.wait_ge(probs_done, a * UNITS + (u + 1))
                for i in range(BU):
                    mm = pe.transpose(turn_ps[:, i * S:(i + 1) * S], probs[:, u, i, :], ident[:, :])
                mm.then_inc(turned, 1)

            def pv(a, u):
                j, t = u % HP, u // HP
                pe.wait_ge(turn_copied, a * UNITS + (u + 1))
                if u:
                    pe.wait_ge(at_split, a * UNITS + u)
                for i in range(BU):
                    b = t * BU + i
                    mm = pe.matmul(pv_ps[:, i * S:(i + 1) * S], v_sb[:, b, j * DH:(j + 1) * DH], probs_t[:, i, :],
                                   start=True, stop=True)
                mm.then_inc(pv_done, 1)

            def out_proj(p, b, projected):
                pe.wait_ge(at_split, p * UNITS - (HP if b < BU else 0))
                if b < BANKS:
                    if projected:
                        pe.wait_ge(proj_copied, p * PROJ + (QK + b + 1))
                    else:
                        pe.wait_ge(acc_done, p * B + (b + 1 + BANKS - B))
                else:
                    pe.wait_ge(acc_done, p * B + (b + 1 - BANKS))
                mm = split_product(proj_ps[b % BANKS][:, :], lambda s, j: at2[s][:, j, b * P:(b + 1) * P],
                                   lambda s, j: w2[s][:, WO, j * D:(j + 1) * D], HP)
                mm.then_inc(out_done, 1)
                return mm

            def turn_xn(i):
                pe.wait_ge(xn_done, i + 1)
                if i >= 2:
                    pe.wait_ge(xt_lo_done, i - 1)
                for c in range(C):
                    mm = pe.transpose(score_ps[i % 2][:, c * P:(c + 1) * P], xn[:, i % G, c * P:(c + 1) * P], ident[:, :])
                mm.then_inc(xt_turned, 1)

            pe.wait_ge(w_lo_done[WK], 1)
            for m in range(UNITS):
                q_or_k(2 * m + 1, m, (lambda c: pe.wait_ge(ctx_lo_done, c + 1)) if m == 0 else None)
            pe.wait_ge(ident_done, 1)
            pe.wait_ge(w_lo_done[WV], 1)
            for g in range(2):
                for m in range(g * VC // 2, (g + 1) * VC // 2):
                    pe.wait_ge(proj_copied, m + 1)
                    v_pair(m, m)
                for i in range(g * G, (g + 1) * G):
                    turn_xn(i)
            pe.wait_ge(w_lo_done[WQ], 1)
            for m in range(UNITS):
                pe.wait_ge(proj_copied, UNITS + m + 1)
                pe.wait_ge(xt_lo_done, (m // HP + 1) * G)
                q_or_k(2 * m, m)

            def iteration(p):
                a = p - 1

                def chunk(n):
                    if n < BANKS:
                        pe.wait_ge(acc_done, (p - 1) * B + (B - BANKS + n + 1))
                    else:
                        pe.wait_ge(proj_copied, p * PROJ + (n - BANKS + 1))
                    if n == 0:
                        pe.wait_ge(w_lo_done[WQ], p + 1)
                    if n == 1:
                        pe.wait_ge(w_lo_done[WK], p + 1)
                    if n == QK:
                        pe.wait_ge(w_lo_done[WV], p + 1)
                    return q_or_k(n, n % BANKS) if n < QK else v_pair(n - QK, n % BANKS)

                pe.wait_ge(proj_copied, p * PROJ)
                scores(a, 0)
                scores(a, 1)
                for n in (0, 1, 2):
                    chunk(n)
                turn(a, 0)
                scores(a, 2)
                chunk(3)
                pv(a, 0)
                turn(a, 1)
                scores(a, 3)
                chunk(4)
                pv(a, 1)
                chunk(5)
                turn(a, 2)
                chunk(6)
                pv(a, 2)
                turn(a, 3)
                chunk(7)
                pv(a, 3)
                for n in range(QK, PROJ):
                    chunk(n)
                pe.wait_ge(w_lo_done[WO], p)
                for b in range(B):
                    out_proj(p, b, True)

            with pe.Fori(1, NPH) as p:
                iteration(p)

            last = NPH - 1
            pe.wait_ge(proj_copied, NPH * PROJ)
            for u in range(UNITS):
                scores(last, u)
            turn(last, 0)
            pv(last, 0)
            turn(last, 1)
            pv(last, 1)
            pe.wait_ge(w_lo_done[WO], NPH)
            out_proj(NPH, 0, False)
            out_proj(NPH, 1, False)
            turn(last, 2)
            out_proj(NPH, 2, False)
            pv(last, 2)
            turn(last, 3)
            out_proj(NPH, 3, False)
            pv(last, 3)
            for b in range(BU, B):
                out_proj(NPH, b, False)

            def turn_xf(i):
                pe.wait_ge(xf_done, i + 1)
                if i >= 2:
                    pe.wait_ge(xf_lo_done, i - 1)
                for c in range(C):
                    mm = pe.transpose(score_ps[i % 2][:, c * P:(c + 1) * P], xf[:, i % G, c * P:(c + 1) * P], ident[:, :])
                mm.then_inc(xf_turned, 1)

            def rows(i):
                return lambda s, c: xt2[s][:, c, i * P:(i + 1) * P]

            def logits(i):
                pe.wait_ge(xf_lo_done, i + 1)
                if i >= G:
                    pe.wait_ge(hg_done, G)
                split_product(lg_ps(i), rows(i), lambda s, c: lg_w[s][:, c, :], C).then_inc(logits_done, 1)

            def base(i):
                if i >= 3:
                    pe.wait_ge(final_done, i - 2)
                else:
                    pe.wait_ge(acc_done, B * (NPH + 1))
                pe.wait_ge(xf_lo_done, i + 1)
                o = proj_ps[i % 3][:, :]
                for c in range(C):
                    for m, (l, r) in enumerate(((0, 0), (1, 0), (0, 1))):
                        pe.matmul(o, rows(i)(l, c), base_w[r][:, c, :], start=(c == 0 and m == 0), stop=False)

            def turn_hg(n):
                pe.wait_ge(hg_done, 2 * n + 2)
                if n:
                    pe.wait_ge(hg_lo_done, n)
                for i in range(2):
                    for e in range(2):
                        mm = pe.transpose(hgt_ps[:, i, e, :], hg[:, (2 * n + i) % G, e * ERH:(e + 1) * ERH], ident[:, :])
                mm.then_inc(hg_turned, 1)

            def lora(i):
                pe.wait_ge(hg_lo_done, i // 2 + 1)
                o = proj_ps[i % 3][:, :]
                for e in range(2):
                    for m, (l, r) in enumerate(((0, 0), (1, 0), (0, 1))):
                        mm = pe.matmul(o, (hgt_hi, hgt_lo)[l][:, i % 2, e, :], lb_w[r][:, e, :], start=False, stop=(e == 1 and m == 2))
                mm.then_inc(ffn_done, 1)

            for k in (WQ, WK, WV):
                pe.wait_ge(w_lo_done[k], NPH + 1)
            for i in range(G):
                turn_xf(i)
            for i in range(G):
                logits(i)
            for i in range(G, B):
                turn_xf(i)
            for i in range(3):
                base(i)
            turn_hg(0)
            for i in range(G, B):
                logits(i)
            pe.wait_ge(w_lo_done[WO], NPH + 1)
            lora(0)
            lora(1)
            turn_hg(1)
            base(3)
            lora(2)
            lora(3)
            base(4)
            base(5)
            turn_hg(2)
            base(6)
            lora(4)
            lora(5)
            turn_hg(3)
            base(7)
            lora(6)
            lora(7)


def kernel(**inputs):
    import numpy as np
    import concourse.bacc as bacc
    from concourse.bass_utils import run_bass_kernel_spmd

    a = {k: np.asarray(v) for k, v in inputs.items()}

    def by_phase(w):
        return w.reshape(NPH, HP, DH, C, P).transpose(0, 4, 3, 1, 2).reshape(NPH, P, WN)

    weights = np.zeros((NPH + 1, 4, P, WN), np.float32)
    for k, name in ((WQ, "w_q"), (WK, "w_k"), (WV, "w_v")):
        weights[:NPH, k] = by_phase(a["L0_xattn_" + name])
    weights[:NPH, WO] = a["L0_xattn_w_out"].reshape(D, NPH, HP, DH).transpose(1, 3, 2, 0).reshape(NPH, P, HP * D)
    base = a["L0_ffn_base_W"].T.reshape(C, P, D).transpose(1, 0, 2).reshape(P, 2, WN)
    weights[NPH, 0:2] = base.transpose(1, 0, 2)
    lg = np.zeros((D, LG), np.float32)
    lg[:, :ER] = a["L0_ffn_lora_A"].reshape(ER, D).T
    lg[:, ER:ER + E] = a["L0_ffn_gate_W"].T
    weights[NPH, 2] = lg.reshape(C, P, LG).transpose(1, 0, 2).reshape(P, WN)
    lb = a["L0_ffn_lora_B"].transpose(0, 2, 1).reshape(2, ERH, D)
    weights[NPH, 3, :ERH] = lb.transpose(1, 0, 2).reshape(ERH, WN)

    arrays = {
        "x": a["x"],
        "ctx_t": np.ascontiguousarray(a["ctx_4096"].reshape(T, D).T).reshape(C, P, T),
        "weights": weights,
        "bias": np.ascontiguousarray(a["L0_xattn_position_bias"].reshape(NPH, HP, S, S).transpose(0, 2, 1, 3)),
        "mask": np.ascontiguousarray(a["mask_BxSxS2_bk0"]),
        "g_x": a["g_xattn"], "g_f": a["g_ffn"], "ln_w": a["L0_xattn_ln_weight"],
    }
    nc = bacc.Bacc("TRN2", target_bir_lowering=False, num_devices=1)
    args = [nc.dram_tensor("in_" + n, v.shape, mybir.dt.from_np(v.dtype), kind="ExternalInput").ap() for n, v in arrays.items()]
    out = nc.dram_tensor("out", (B, S, D), F32, kind="ExternalOutput").ap()
    build(nc, *args, out)
    r = run_bass_kernel_spmd(nc, [{"in_" + n: v for n, v in arrays.items()}], core_ids=[0])
    return r.results[0]["out"]
```

```python
from contextlib import ExitStack

import concourse.bass as bass
from concourse import mybir

F32 = mybir.dt.float32
F32R = mybir.dt.float32r
U8 = mybir.dt.uint8
U32 = mybir.dt.uint32
ALU = mybir.AluOpType
ACT = mybir.ActivationFunctionType
AX = mybir.AxisListType

P = 128
B, S, D = 8, 128, 512
H, DH = 32, 128
E, R, TOP = 28, 8, 2
SCALING = 16 / R
EPS = 1e-5
NEG = -1e30
T = B * S
C = D // P
HP = 2
NPH = H // HP
HALF = T // 2
UNITS = HP * 2
BU = B // 2
QK = 2 * UNITS
VC = B // 2
PROJ = QK + VC
BANKS = 4
WQ, WK, WV, WO = range(4)
WN = C * HP * DH
ER = E * R
Q32 = 32
ERH = ER // 2
G = B // 2
LG = 256


def build(nc, x, ctx_t, weights, bias, mask, g_x, g_f, ln_w, out):
    ctx = ExitStack()
    with ctx:
        def sb(name, shape, dt=F32):
            return ctx.enter_context(nc.sbuf_tensor(name, shape, dt))

        def sem(name):
            return ctx.enter_context(nc.semaphore(name))

        def bank(name):
            return ctx.enter_context(nc.psum_tensor(name, [P, 512], F32))

        xt_hi, xt_lo = sb("xt_hi", [P, C, T], F32R), sb("xt_lo", [P, C, T], F32R)
        ct_hi, ct_lo = sb("ct_hi", [P, C, T], F32R), sb("ct_lo", [P, C, T], F32R)
        w_hi, w_lo = sb("w_hi", [P, 4, WN], F32R), sb("w_lo", [P, 4, WN], F32R)
        w_raw = sb("w_raw", [P, 4, WN])
        qt, kt = sb("qt", [P, HP, T]), sb("kt", [P, HP, T])
        v_sb = sb("v_sb", [P, B, HP * DH])
        at_hi, at_lo = sb("at_hi", [P, HP, T], F32R), sb("at_lo", [P, HP, T], F32R)
        acc = sb("acc", [P, B, D])
        bias_sb = sb("bias_sb", [P, HP, S])
        comb = sb("comb", [P, HP, B, S])
        mask_u8 = sb("mask_u8", [P, B, S], U8)
        mask_add = sb("mask_add", [P, B, S])
        row_any = sb("row_any", [P, B])
        probs = sb("probs", [P, UNITS, BU, S])
        probs_t = sb("probs_t", [P, 2, BU, S])
        neg_max, row_sum, row_scale = (sb(n, [P, UNITS, BU]) for n in ("neg_max", "row_sum", "row_scale"))
        ident = sb("ident", [P, P])
        lnw = sb("lnw", [P, D])
        gates = sb("gates", [P, 2])
        tanh_g = sb("tanh_g", [P, 2])
        stats = sb("stats", [P, B, 6])
        mean_var = sb("mean_var", [P, B, 2])
        pow_half = sb("pow_half", [P, B])
        var_e, rstd, newton = sb("var_e", [P, B]), sb("rstd", [P, B]), sb("newton", [P, B])
        rms = sb("rms", [P, B])
        shift = sb("shift", [P, B])
        warm = sb("warm", [P, 1])
        expert_id = sb("expert_id", [P, E])
        top_v, top_i, top_f = sb("top_v", [P, B, 8]), sb("top_i", [P, B, 8], U32), sb("top_f", [P, B, 8])
        gap, e_gap, gate1, gate2 = (sb(n, [P, B]) for n in ("gap", "e_gap", "gate1", "gate2"))
        pick1, pick2 = sb("pick1", [P, G, E]), sb("pick2", [P, G, E])
        hg = sb("hg", [P, G, ER])
        hgt_hi, hgt_lo = sb("hgt_hi", [ERH, 2, 2, P], F32R), sb("hgt_lo", [ERH, 2, 2, P], F32R)

        score_ps = [bank(f"score_ps{i}") for i in range(2)]
        turn_ps, pv_ps = bank("turn_ps"), bank("pv_ps")
        proj_ps = [bank(f"proj_ps{i}") for i in range(BANKS)]

        ctx_raw = [t[:, i, :] for t in (qt, kt) for i in range(HP)]
        xn = comb[:, :, :, :].rearrange("p h (a b) s -> p (h a) (b s)", b=D // S)
        xf = v_sb[:, :, :].rearrange("p (i n) d -> p i (n d)", n=2)
        result = probs[:, :, :, :].rearrange("p n b s -> p n (b s)")
        x_again = [w_raw[:, i // 2, (i % 2) * D:(i % 2 + 1) * D] for i in range(6)] + [qt[:, 0, i * D:(i + 1) * D] for i in range(2)]
        base_w = [w[:, 0:2, :].rearrange("p a (c n) -> p (a c) n", n=D) for w in (w_hi, w_lo)]
        lg_w = [w[:, 2, :].rearrange("p (c n) -> p c n", n=LG) for w in (w_hi, w_lo)]
        lb_w = [w[0:ERH, 3, :].rearrange("p (e n) -> p e n", n=D) for w in (w_hi, w_lo)]

        xn_ps = [score_ps[0], score_ps[1], turn_ps, pv_ps]
        at_last = (ct_hi, ct_lo)
        wo_last = (ct_hi[:, HP, :], ct_lo[:, HP, :])
        LAST = NPH - 1

        def pv_bank(a, u):
            return pv_ps if isinstance(a, int) and a == LAST else (pv_ps, turn_ps)[u % 2]

        def half(t):
            return slice(t * HALF, (t + 1) * HALF)

        def lg_ps(i):
            return (turn_ps, pv_ps)[i % G // 2][:, (i % 2) * LG:(i % 2 + 1) * LG]

        hgt_ps = proj_ps[3][0:ERH, :].rearrange("p (i e s) -> p i e s", i=2, e=2)

        x_in = [sem(f"x_in{i}") for i in range(4)]
        ctx_in = [[sem(f"ctx_in{c}_{t}") for c in range(C)] for t in range(2)]
        w_in = [sem(f"w_in{k}") for k in range(4)]
        wk_half_in, wk_half_hi, wk_half_lo = sem("wk_half_in"), sem("wk_half_hi"), sem("wk_half_lo")
        bias_in, mask_in, small_in = sem("bias_in"), sem("mask_in"), sem("small_in")
        x2_in = [sem(f"x2_in{i}") for i in range(B)]
        stored = [sem(f"stored{i}") for i in range(UNITS)]
        w_hi_done = [sem(f"w_hi_done{k}") for k in range(4)]
        w_lo_done = [sem(f"w_lo_done{k}") for k in range(4)]
        ctx_hi_done, ctx_lo_done = sem("ctx_hi_done"), sem("ctx_lo_done")
        ident_zero, ident_done, pow_const, ids_done = sem("ident_zero"), sem("ident_done"), sem("pow_const"), sem("ids_done")
        dve_step = sem("dve_step")
        var_done, rstd0_done = sem("var_done"), sem("rstd0_done")
        xn_done, xt_turned = sem("xn_done"), sem("xt_turned")
        xt_hi_done, xt_lo_done = sem("xt_hi_done"), sem("xt_lo_done")
        acc_done = sem("acc_done")
        mask_done, comb_done, tanh_done = sem("mask_done"), sem("comb_done"), sem("tanh_done")
        proj_done, proj_copied = sem("proj_done"), sem("proj_copied")
        scores_done, biased, max_done = sem("scores_done"), sem("biased"), sem("max_done")
        exp_done, scaled, probs_done = sem("exp_done"), sem("scaled"), sem("probs_done")
        turned, turn_copied = sem("turned"), sem("turn_copied")
        pv_done, at_hi_done, at_split = sem("pv_done"), sem("at_hi_done"), sem("at_split")
        out_done, first_share = sem("out_done"), sem("first_share")
        resid_done, shift_done = sem("resid_done"), sem("shift_done")
        xf_done, xf_turned, xf_hi_done, xf_lo_done = sem("xf_done"), sem("xf_turned"), sem("xf_hi_done"), sem("xf_lo_done")
        logits_done, gap_done, e_gap_done = sem("logits_done"), sem("gap_done"), sem("e_gap_done")
        hg_done, hg_turned, hg_hi_done, hg_lo_done = sem("hg_done"), sem("hg_turned"), sem("hg_hi_done"), sem("hg_lo_done")
        ffn_done, final_done = sem("ffn_done"), sem("final_done")

        block = ctx.enter_context(nc.Block())

        @block.sync
        def _(sp):
            def load_w(k, p):
                sp.dma_start(w_raw[:, k, :], weights[p, k] if isinstance(p, int)
                             else weights[bass.ds(p, 1), k].rearrange("a p n -> p (a n)")).then_inc(w_in[k], 16)

            def load_x(i):
                sp.dma_start(acc[:, 2 * i:2 * i + 2, :], x[2 * i:2 * i + 2].rearrange("b s d -> s b d")).then_inc(x_in[i], 16)

            def load_ctx(c, t):
                sp.dma_start(ctx_raw[c][:, half(t)], ctx_t[c][:, half(t)]).then_inc(ctx_in[t][c], 16)

            sp.dma_start(w_raw[:, WK, 0:WN // 2], weights[0, WK][:, 0:WN // 2]).then_inc(wk_half_in, 16)
            load_ctx(0, 0)
            load_ctx(1, 0)
            sp.dma_start(w_raw[:, WK, WN // 2:WN], weights[0, WK][:, WN // 2:WN]).then_inc(w_in[WK], 16)
            load_ctx(2, 0)
            load_ctx(3, 0)
            for c in range(C):
                load_ctx(c, 1)
            load_x(0)
            load_x(1)
            load_w(WV, 0)
            load_x(2)
            load_x(3)
            sp.dma_start(lnw[:, :], ln_w.rearrange("(a n) -> a n", a=1).to_broadcast([P, D])).then_inc(small_in, 16)
            sp.dma_start(gates[:, 0:1], g_x.rearrange("(a n) -> a n", a=1).to_broadcast([P, 1])).then_inc(small_in, 16)
            sp.dma_start(gates[:, 1:2], g_f.rearrange("(a n) -> a n", a=1).to_broadcast([P, 1])).then_inc(small_in, 16)
            load_w(WQ, 0)
            sp.dma_start(mask_u8[:, :, :], mask.rearrange("b q k -> q b k")).then_inc(mask_in, 16)
            sp.dma_start(bias_sb[:, :, :], bias[0]).then_inc(bias_in, 16)
            load_w(WO, 0)

            def refill(p):
                for k in (WQ, WK, WV):
                    sp.wait_ge(w_lo_done[k], p + 1)
                    load_w(k, p + 1)

            def refill_out(p):
                sp.wait_ge(w_lo_done[WO], p + 1)
                load_w(WO, p + 1)

            with sp.Fori(0, NPH - 1) as p:
                refill(p)
                sp.wait_ge(comb_done, p * HP + HP)
                sp.dma_start(bias_sb[:, :, :], bias[bass.ds(p + 1, 1)].rearrange("a q h k -> q (a h) k")).then_inc(bias_in, 16)
                refill_out(p)
            refill(LAST)

            def load_x_again(i):
                sp.wait_ge(w_lo_done[i // 2], NPH + 1)
                sp.dma_start(x_again[i], x[i]).then_inc(x2_in[i], 16)

            for i in range(G):
                load_x_again(i)
            refill_out(LAST)
            for i in range(G, 6):
                load_x_again(i)
            sp.wait_ge(scores_done, UNITS * NPH)
            for i in range(6, B):
                sp.dma_start(x_again[i], x[i]).then_inc(x2_in[i], 16)
            for i in range(B):
                sp.wait_ge(final_done, i + 1)
                sp.dma_start(out[i], result[:, i % UNITS, :]).then_inc(stored[i % UNITS], 16)
            for s in stored:
                sp.wait_ge(s, 16 * (B // UNITS))

        @block.gpsimd
        def _(pool):
            pool.memset(ident[:, :], 0.0).then_inc(ident_zero, 1)
            pool.wait_ge(ident_zero, 1)
            pool.affine_select(out=ident[:, :], in_=ident[:, :], compare_op=ALU.not_equal, fill=1.0, base=0,
                               pattern=[[-1, P]], channel_multiplier=1).then_inc(ident_done, 1)
            pool.memset(pow_half[:, :], -0.5).then_inc(pow_const, 1)
            pool.iota(expert_id[:, :], pattern=[[1, E]], base=0, channel_multiplier=0,
                      allow_small_or_imprecise_dtypes=True).then_inc(ids_done, 1)

            def rest(k, p, hi=None, lo=None):
                hi, lo = (w_hi[:, k, :], w_lo[:, k, :]) if hi is None else (hi, lo)
                pool.wait_ge(w_hi_done[k], p + 1)
                pool.tensor_tensor(lo, w_raw[:, k, :], hi.bitcast(F32), ALU.subtract).then_inc(w_lo_done[k], 1)

            def add_mask(p, first):
                pool.wait_ge(bias_in, (p + 1) * 16)
                for j in range(HP):
                    if first:
                        pool.wait_ge(xt_turned, G + (j + 1) * (G // HP))
                    else:
                        pool.wait_ge(biased, (p - 1) * UNITS + (HP + j + 1))
                    pool.tensor_tensor(comb[:, j, :, :], mask_add[:, :, :],
                                       bias_sb[:, j:j + 1, :].to_broadcast([P, B, S]), ALU.add).then_inc(comb_done, 1)

            def inverse_root(n, v, r):
                pool.wait_ge(var_done, n)
                pool.tensor_tensor(r, v, pow_half[:, 0:G], ALU.pow).then_inc(rstd0_done, 1)

            pool.wait_ge(pow_const, 1)
            for g in range(2):
                at = slice(g * G, (g + 1) * G)
                inverse_root(2 * g + 1, var_e[:, at], rstd[:, at])
                inverse_root(2 * g + 2, var_e[:, at], rms[:, at])
            rest(WQ, 0)
            pool.wait_ge(mask_done, 1)
            add_mask(0, True)
            for k in (WK, WV):
                rest(k, 1)
            rest(WO, 0)
            with pool.Fori(1, LAST) as p:
                add_mask(p, False)
                for k in (WQ, WK, WV):
                    rest(k, p + 1)
                rest(WO, p)
            add_mask(LAST, False)
            rest(WQ, NPH)
            rest(WK, NPH)
            rest(WO, LAST, *wo_last)
            rest(WV, NPH)
            for g in range(2):
                at = slice(g * G, (g + 1) * G)
                inverse_root(5 + g, var_e[:, at], rstd[:, at])
                if g == 0:
                    rest(WO, NPH)

        @block.scalar
        def _(act):
            def lead(k, p, hi=None):
                act.wait_ge(w_in[k], (p + 1) * 16)
                act.activation(w_hi[:, k, :] if hi is None else hi, w_raw[:, k, :], ACT.Copy).then_inc(w_hi_done[k], 1)

            def copy_proj(p, n, i, dst):
                act.wait_ge(proj_done, p * PROJ + (n + 1))
                act.activation(dst, proj_ps[i][:, :], ACT.Copy).then_inc(proj_copied, 1)

            def q_or_k(m):
                u, t = m // 2, (qt, kt)[m % 2]
                return t[:, u % HP, (u // HP) * HALF:(u // HP + 1) * HALF]

            def v_dst(m):
                return v_sb[:, 2 * m:2 * m + 2, :].rearrange("p b d -> p (b d)")

            def exps(a, u):
                act.wait_ge(max_done, a * UNITS + (u + 1))
                for i in range(BU):
                    e = act.activation(probs[:, u, i, :], probs[:, u, i, :], ACT.Exp,
                                       bias=neg_max[:, u, i:i + 1], accum_out=row_sum[:, u, i:i + 1])
                e.then_inc(exp_done, 1)

            def lead_at(a, u, hi=at_hi):
                act.wait_ge(pv_done, a * UNITS + (u + 1))
                act.activation(hi[:, u % HP, half(u // HP)], pv_bank(a, u)[:, :], ACT.Copy).then_inc(at_hi_done, 1)

            def lead_xt(i):
                act.wait_ge(xt_turned, i + 1)
                act.activation(xt_hi[:, :, i * P:(i + 1) * P], xn_ps[i % G][:, :].rearrange("p (c s) -> p c s", c=C),
                               ACT.Copy).then_inc(xt_hi_done, 1)

            act.wait_ge(pow_const, 1)
            act.activation(warm[:, :], pow_half[:, 0:1], ACT.Exp)
            def lead_ctx(c, t):
                act.wait_ge(ctx_in[t][c], 16)
                act.activation(ct_hi[:, c, half(t)], ctx_raw[c][:, half(t)], ACT.Copy).then_inc(ctx_hi_done, 1)

            act.wait_ge(wk_half_in, 16)
            act.activation(w_hi[:, WK, 0:WN // 2], w_raw[:, WK, 0:WN // 2], ACT.Copy).then_inc(wk_half_hi, 1)
            lead_ctx(0, 0)
            lead_ctx(1, 0)
            act.wait_ge(w_in[WK], 16)
            act.activation(w_hi[:, WK, WN // 2:WN], w_raw[:, WK, WN // 2:WN], ACT.Copy).then_inc(w_hi_done[WK], 1)
            lead_ctx(2, 0)
            lead_ctx(3, 0)
            for c in range(C):
                lead_ctx(c, 1)
            for m in range(2):
                copy_proj(0, m, m, q_or_k(2 * m + 1))
            lead(WV, 0)
            for m in range(2, UNITS):
                copy_proj(0, m, m, q_or_k(2 * m + 1))
            for m in range(2):
                copy_proj(0, UNITS + m, m, v_dst(m))
            act.wait_ge(small_in, 48)
            act.activation(tanh_g[:, :], gates[:, :], ACT.Tanh).then_inc(tanh_done, 1)
            lead(WQ, 0)
            lead_xt(0)
            lead_xt(1)
            lead_xt(2)
            lead_xt(3)
            copy_proj(0, UNITS + 2, 2, v_dst(2))
            copy_proj(0, UNITS + 3, 0, q_or_k(0))
            for i in range(G, B):
                lead_xt(i)
            for m in range(1, UNITS):
                copy_proj(0, UNITS + 3 + m, m % 3, q_or_k(2 * m))
            lead(WQ, 1)
            copy_proj(0, PROJ - 1, 3, v_dst(3))
            for k in (WK, WV):
                lead(k, 1)
            lead(WO, 0)

            def iteration(p):
                a = p - 1

                def chunk(n):
                    copy_proj(p, n, n % BANKS, q_or_k(n) if n < QK else v_dst(n - QK))

                exps(a, 0)
                chunk(0)
                exps(a, 1)
                chunk(1)
                chunk(2)
                exps(a, 2)
                chunk(3)
                lead_at(a, 0)
                exps(a, 3)
                chunk(4)
                chunk(5)
                lead_at(a, 1)
                chunk(6)
                chunk(7)
                if isinstance(p, int):
                    return
                chunk(QK)
                lead_at(a, 2)
                chunk(QK + 1)
                lead_at(a, 3)
                chunk(QK + 2)
                chunk(QK + 3)
                for k in (WQ, WK, WV):
                    lead(k, p + 1)
                act.wait_ge(out_done, p * B)
                lead(WO, p)

            with act.Fori(1, LAST) as p:
                iteration(p)
            iteration(LAST)

            def last_v(m):
                copy_proj(LAST, QK + m, m, v_dst(m))

            lead(WQ, NPH)
            lead(WK, NPH)
            last_v(0)
            lead_at(LAST - 1, 2)
            exps(LAST, 0)
            last_v(1)
            lead_at(LAST - 1, 3)
            last_v(2)
            exps(LAST, 1)
            last_v(3)
            lead(WO, LAST, wo_last[0])
            lead_at(LAST, 0, at_last[0])
            exps(LAST, 2)
            lead(WV, NPH)
            lead_at(LAST, 1, at_last[0])
            exps(LAST, 3)
            lead_at(LAST, 2, at_last[0])
            lead_at(LAST, 3, at_last[0])

            def norm_xf(i):
                act.wait_ge(shift_done, i // G + 1)
                if i >= G:
                    act.wait_ge(xf_turned, i - G + 1)
                act.activation(xf[:, i % G, :], acc[:, i, :], ACT.Identity, bias=shift[:, i:i + 1],
                               scale=rstd[:, i:i + 1]).then_inc(xf_done, 1)

            def lead_xf(i):
                act.wait_ge(xf_turned, i + 1)
                act.activation(xt_hi[:, :, i * P:(i + 1) * P], score_ps[i % 2][:, :].rearrange("p (c s) -> p c s", c=C),
                               ACT.Copy).then_inc(xf_hi_done, 1)

            def exp_gap(g):
                act.wait_ge(gap_done, g + 1)
                act.activation(e_gap[:, g * G:(g + 1) * G], gap[:, g * G:(g + 1) * G], ACT.Exp).then_inc(e_gap_done, 1)

            def lead_hg(n):
                act.wait_ge(hg_turned, n + 1)
                if n:
                    act.wait_ge(ffn_done, 2 * n)
                act.activation(hgt_hi[:, :, :, :], hgt_ps, ACT.Copy).then_inc(hg_hi_done, 1)

            for i in range(G):
                norm_xf(i)
            for i in range(G):
                lead_xf(i)
            act.wait_ge(first_share, B)
            lead(WO, NPH)
            norm_xf(G)
            exp_gap(0)
            for i in range(G + 1, B):
                norm_xf(i)
            for i in range(G, B):
                lead_xf(i)
            lead_hg(0)
            exp_gap(1)
            for n in range(1, B // 2):
                lead_hg(n)

        @block.vector
        def _(dve):
            steps = [0]

            def ordered(ins):
                steps[0] += 1
                ins.then_inc(dve_step, 1)
                dve.wait_ge(dve_step, steps[0])

            def refine(n, r, v, t):
                dve.wait_ge(rstd0_done, n)
                ordered(dve.tensor_tensor(t, r, r, ALU.mult))
                ordered(dve.scalar_tensor_tensor(out=t, in0=t, scalar=-0.5, in1=v, op0=ALU.mult, op1=ALU.mult))
                ordered(dve.scalar_tensor_tensor(out=r, in0=t, scalar=1.5, in1=r, op0=ALU.add, op1=ALU.mult))

            def variances(i0):
                for i in range(i0, i0 + G):
                    ordered(dve.bn_aggr(mean_var[:, i, :], stats[:, i, :]))
                dve.tensor_scalar(var_e[:, i0:i0 + G], mean_var[:, i0:i0 + G, 1], EPS, None, ALU.add).then_inc(var_done, 1)

            def rest_ctx(c, t):
                dve.wait_ge(ctx_hi_done, t * C + c + 1)
                dve.tensor_tensor(ct_lo[:, c, half(t)], ctx_raw[c][:, half(t)], ct_hi[:, c, half(t)].bitcast(F32),
                                  ALU.subtract).then_inc(ctx_lo_done, 1)

            def rest_w(k, at, hi_done, lo_done, p=0):
                dve.wait_ge(hi_done, p + 1)
                dve.tensor_tensor(w_lo[:, k, at], w_raw[:, k, at], w_hi[:, k, at].bitcast(F32), ALU.subtract).then_inc(lo_done, 1)

            rest_w(WK, slice(0, WN // 2), wk_half_hi, wk_half_lo)
            rest_ctx(0, 0)
            rest_ctx(1, 0)
            rest_w(WK, slice(WN // 2, WN), w_hi_done[WK], w_lo_done[WK])
            rest_ctx(2, 0)
            rest_ctx(3, 0)
            for c in range(C):
                rest_ctx(c, 1)

            def rest_xt(i, hi_done, lo_done, banks):
                dve.wait_ge(hi_done, i + 1)
                dve.tensor_tensor(xt_lo[:, :, i * P:(i + 1) * P], banks[i % len(banks)][:, :].rearrange("p (c s) -> p c s", c=C),
                                  xt_hi[:, :, i * P:(i + 1) * P].bitcast(F32), ALU.subtract).then_inc(lo_done, 1)

            def group(g):
                return slice(g * G, (g + 1) * G), range(g * G, (g + 1) * G)

            def x_stats(n):
                dve.wait_ge(x_in[n], 16)
                for i in (2 * n, 2 * n + 1):
                    st = dve.bn_stats(stats[:, i, :], acc[:, i, :])
                return st

            def rms_variances(g):
                at, _ = group(g)
                refine(2 * g + 1, rstd[:, at], var_e[:, at], newton[:, at])
                ordered(dve.tensor_tensor(newton[:, at], rstd[:, at], rstd[:, at], ALU.mult))
                ordered(dve.tensor_tensor(newton[:, at], newton[:, at], mean_var[:, at, 1], ALU.mult))
                dve.tensor_scalar(var_e[:, at], newton[:, at], EPS, None, ALU.add).then_inc(var_done, 1)

            def rms_root(g):
                at, _ = group(g)
                refine(2 * g + 2, rms[:, at], var_e[:, at], newton[:, at])

            def norm_x(g, tiles):
                def layer(i):
                    dve.tensor_scalar(acc[:, i, :], acc[:, i, :], mean_var[:, i, 0:1], rstd[:, i:i + 1],
                                      ALU.subtract, ALU.mult).then_inc(acc_done, 1)

                layer(tiles[0])
                for i in tiles:
                    if i + 1 in tiles:
                        layer(i + 1)
                    dve.wait_ge(acc_done, i + 1)
                    if g:
                        dve.wait_ge(xt_turned, i - G + 1)
                    dve.scalar_tensor_tensor(out=xn[:, i % G, :], in0=acc[:, i, :], scalar=rms[:, i:i + 1], in1=lnw[:, :],
                                             op0=ALU.mult, op1=ALU.mult).then_inc(xn_done, 1)

            x_stats(0)
            ordered(x_stats(1))
            variances(0)
            x_stats(2)
            rest_w(WV, slice(0, WN), w_hi_done[WV], w_lo_done[WV])
            rms_variances(0)
            ordered(x_stats(3))
            variances(G)
            rms_root(0)
            dve.wait_ge(small_in, 48)
            norm_x(0, range(G // 2))
            rms_variances(1)
            norm_x(0, range(G // 2, G))
            for i in range(G):
                rest_xt(i, xt_hi_done, xt_lo_done, xn_ps)
            rms_root(1)
            norm_x(1, range(G, B))
            for i in range(G, B):
                rest_xt(i, xt_hi_done, xt_lo_done, xn_ps)
            dve.wait_ge(mask_in, 16)
            dve.tensor_scalar(mask_add[:, :, :], mask_u8[:, :, :], 1.0, -NEG, ALU.subtract, ALU.mult).then_inc(mask_done, 1)
            ordered(dve.tensor_reduce(row_any[:, :], mask_u8[:, :, :], AX.X, ALU.max))
            rest_w(WQ, slice(0, WN), w_hi_done[WQ], w_lo_done[WQ], 1)

            def add_bias(a, u):
                j, t = u % HP, u // HP
                dve.wait_ge(scores_done, a * UNITS + (u + 1))
                dve.wait_ge(comb_done, a * HP + (j + 1))
                dve.tensor_tensor(probs[:, u, :, :], score_ps[u % 2][:, :].rearrange("p (b s) -> p b s", b=BU),
                                  comb[:, j, t * BU:(t + 1) * BU, :], ALU.add).then_inc(biased, 1)
                dve.wait_ge(biased, a * UNITS + (u + 1))
                dve.tensor_reduce(neg_max[:, u, :], probs[:, u, :, :], AX.X, ALU.max, negate=True).then_inc(max_done, 1)

            def normalise(a, u):
                t = u // HP
                dve.wait_ge(exp_done, a * UNITS + (u + 1))
                dve.reciprocal(row_scale[:, u, :], row_sum[:, u, :]).then_inc(scaled, 1)
                dve.wait_ge(scaled, a * (2 * UNITS) + (2 * u + 1))
                dve.tensor_tensor(row_scale[:, u, :], row_scale[:, u, :], row_any[:, t * BU:(t + 1) * BU],
                                  ALU.mult).then_inc(scaled, 1)
                dve.wait_ge(scaled, a * (2 * UNITS) + (2 * u + 2))
                dve.tensor_tensor(probs[:, u, :, :], probs[:, u, :, :],
                                  row_scale[:, u, :].unsqueeze(2).to_broadcast([P, BU, S]), ALU.mult).then_inc(probs_done, 1)

            def turn_probs(a, u):
                dve.wait_ge(probs_done, a * UNITS + (u + 1))
                if u >= 2:
                    dve.wait_ge(pv_done, a * UNITS + (u - 1))
                for q in range(0, S, Q32):
                    for k in range(0, S, Q32):
                        tr = dve.transpose(probs_t[k:k + Q32, u % 2, :, q:q + Q32], probs[q:q + Q32, u, :, k:k + Q32])
                tr.then_inc(turn_copied, 1)

            def copy_turned(a, u):
                dve.wait_ge(turned, u + 1)
                dve.tensor_copy(probs_t[:, u % 2, :, :], turn_ps[:, :].rearrange("p (b s) -> p b s", b=BU)).then_inc(turn_copied, 1)

            def rest_at(a, u, hi=at_hi, lo=at_lo):
                dve.wait_ge(at_hi_done, a * UNITS + (u + 1))
                to = (slice(0, P), u % HP, half(u // HP))
                dve.tensor_tensor(lo[to], pv_bank(a, u)[:, :], hi[to].bitcast(F32), ALU.subtract).then_inc(at_split, 1)

            def add_out(a, b):
                dve.wait_ge(out_done, a * B + (b + 1))
                dve.tensor_tensor(acc[:, b, :], proj_ps[b % BANKS][:, :], acc[:, b, :], ALU.add).then_inc(acc_done, 1)

            def iteration(a):
                add_bias(a, 0)
                add_bias(a, 1)
                normalise(a, 0)
                turn_probs(a, 0)
                normalise(a, 1)
                add_bias(a, 2)
                turn_probs(a, 1)
                normalise(a, 2)
                add_bias(a, 3)
                rest_at(a, 0)
                turn_probs(a, 2)
                normalise(a, 3)
                rest_at(a, 1)
                turn_probs(a, 3)
                if isinstance(a, int):
                    return
                rest_at(a, 2)
                rest_at(a, 3)
                for b in range(B):
                    add_out(a, b)

            with dve.Fori(0, LAST - 1) as a:
                iteration(a)
            iteration(LAST - 1)

            dve.wait_ge(tanh_done, 1)
            dve.wait_ge(acc_done, B * LAST)

            def residual(i):
                dve.wait_ge(x2_in[i], 16)
                dve.scalar_tensor_tensor(out=acc[:, i, :], in0=acc[:, i, :], scalar=tanh_g[:, 0:1], in1=x_again[i],
                                         op0=ALU.mult, op1=ALU.add).then_inc(resid_done, 1)

            def last_out(i):
                dve.wait_ge(resid_done, i + 1)
                dve.wait_ge(out_done, (LAST - 1) * B + i + 1)
                dve.scalar_tensor_tensor(out=acc[:, i, :], in0=proj_ps[i % BANKS][:, :], scalar=tanh_g[:, 0:1],
                                         in1=acc[:, i, :], op0=ALU.mult, op1=ALU.add).then_inc(acc_done, 1)

            def statistics(i):
                dve.wait_ge(acc_done, B * LAST + i + 1)
                return dve.bn_stats(stats[:, i, :], acc[:, i, :])

            def second_norm(g):
                at = slice(g * G, (g + 1) * G)
                refine(5 + g, rstd[:, at], var_e[:, at], newton[:, at])
                dve.scalar_tensor_tensor(out=shift[:, at], in0=mean_var[:, at, 0], scalar=-1.0, in1=rstd[:, at],
                                         op0=ALU.mult, op1=ALU.mult).then_inc(shift_done, 1)

            def best(g):
                for i in range(g * G, (g + 1) * G):
                    dve.wait_ge(logits_done, i // 2 * 2 + 2)
                    m = dve.max(top_v[:, i, :], lg_ps(i)[:, ER:ER + E])
                ordered(m)
                at = slice(g * G, (g + 1) * G)
                dve.tensor_tensor(gap[:, at], top_v[:, at, 1], top_v[:, at, 0], ALU.subtract).then_inc(gap_done, 1)
                for i in range(g * G, (g + 1) * G):
                    m = dve.max_index(top_i[:, i, :], top_v[:, i, :], lg_ps(i)[:, ER:ER + E])
                ordered(m)
                ordered(dve.tensor_copy(top_f[:, at, :], top_i[:, at, :]))

            def gate(g):
                at = slice(g * G, (g + 1) * G)
                dve.wait_ge(e_gap_done, g + 1)
                ordered(dve.tensor_scalar(gate1[:, at], e_gap[:, at], 1.0, 1.0 / SCALING, ALU.add, ALU.mult))
                ordered(dve.reciprocal(gate1[:, at], gate1[:, at]))
                ordered(dve.tensor_tensor(gate2[:, at], gate1[:, at], e_gap[:, at], ALU.mult))
                for i in range(g * G, (g + 1) * G):
                    dve.tensor_scalar(pick1[:, i % G, :], expert_id[:, :], top_f[:, i, 0:1], gate1[:, i:i + 1], ALU.is_equal, ALU.mult)
                    m = dve.tensor_scalar(pick2[:, i % G, :], expert_id[:, :], top_f[:, i, 1:2], gate2[:, i:i + 1],
                                          ALU.is_equal, ALU.mult)
                ordered(m)
                ordered(dve.tensor_tensor(pick1[:, :, :], pick1[:, :, :], pick2[:, :, :], ALU.add))
                for i in range(g * G, (g + 1) * G):
                    if g:
                        dve.wait_ge(hg_turned, (i - G) // 2 + 1)
                    dve.tensor_tensor(hg[:, i % G, :].rearrange("p (e r) -> p e r", r=R),
                                      lg_ps(i)[:, 0:ER].rearrange("p (e r) -> p e r", r=R),
                                      pick1[:, i % G, :].unsqueeze(2).to_broadcast([P, E, R]), ALU.mult).then_inc(hg_done, 1)

            def rest_hg(n):
                dve.wait_ge(hg_hi_done, n + 1)
                dve.tensor_tensor(hgt_lo[:, :, :, :], hgt_ps, hgt_hi[:, :, :, :].bitcast(F32),
                                  ALU.subtract).then_inc(hg_lo_done, 1)

            def finish(i):
                dve.wait_ge(ffn_done, i + 1)
                if i >= UNITS:
                    dve.wait_ge(stored[i % UNITS], 16 * (i // UNITS))
                dve.scalar_tensor_tensor(out=result[:, i % UNITS, :], in0=proj_ps[i % 3][:, :], scalar=tanh_g[:, 1:2],
                                         in1=acc[:, i, :], op0=ALU.mult, op1=ALU.add).then_inc(final_done, 1)

            def last_rest(u):
                rest_at(LAST, u, *at_last)

            def out_and_statistics(i):
                last_out(i)
                return statistics(i)

            def rest_xf(i):
                rest_xt(i, xf_hi_done, xf_lo_done, score_ps)

            rest_at(LAST - 1, 2)
            add_bias(LAST, 0)
            rest_at(LAST - 1, 3)
            normalise(LAST, 0)
            add_bias(LAST, 1)
            copy_turned(LAST, 0)
            normalise(LAST, 1)
            residual(0)
            add_bias(LAST, 2)
            last_rest(0)
            copy_turned(LAST, 1)
            normalise(LAST, 2)
            residual(1)
            add_bias(LAST, 3)
            last_rest(1)
            residual(2)
            normalise(LAST, 3)
            copy_turned(LAST, 2)
            residual(3)
            out_and_statistics(0)
            last_rest(2)
            last_out(1)
            copy_turned(LAST, 3)
            statistics(1)
            out_and_statistics(2)
            last_rest(3)
            ordered(out_and_statistics(3))
            variances(0)
            residual(4)
            second_norm(0)
            for i in range(5, B):
                residual(i)
            out_and_statistics(4)
            rest_xf(0)
            rest_xf(1)
            out_and_statistics(5)
            rest_xf(2)
            rest_xf(3)
            out_and_statistics(6)
            ordered(out_and_statistics(7))
            variances(G)
            second_norm(1)
            dve.wait_ge(ids_done, 1)
            best(0)
            gate(0)
            for i in range(G, B):
                rest_xf(i)
            rest_hg(0)
            best(1)
            finish(0)
            finish(1)
            rest_hg(1)
            gate(1)
            finish(2)
            finish(3)
            for n in (2, 3):
                rest_hg(n)
                finish(2 * n)
                finish(2 * n + 1)

        @block.tensor
        def _(pe):
            def split_product(o, lhs, rhs, terms, each=None, start=True, stop=True):
                for n in range(terms):
                    if each:
                        each(n)
                    for m, (l, r) in enumerate(((0, 0), (1, 0), (0, 1))):
                        mm = pe.matmul(o, lhs(l, n), rhs(r, n), start=(start and n == 0 and m == 0),
                                       stop=(stop and n == terms - 1 and m == 2))
                return mm

            w2, xt2, ct2, at2 = (w_hi, w_lo), (xt_hi, xt_lo), (ct_hi, ct_lo), (at_hi, at_lo)

            def q_or_k(m, i, each=None):
                u, k, act2 = m // 2, (WQ, WK)[m % 2], (xt2, ct2)[m % 2]
                j = u % HP
                mm = split_product(proj_ps[i][:, :], lambda s, c: w2[s][:, k, c * HP * DH + j * DH:c * HP * DH + (j + 1) * DH],
                                   lambda s, c: act2[s][:, c, half(u // HP)], C, each)
                mm.then_inc(proj_done, 1)

            def v_one(b, i):
                return split_product(proj_ps[i][:, (b % 2) * HP * DH:(b % 2 + 1) * HP * DH],
                                     lambda s, c: ct2[s][:, c, b * P:(b + 1) * P],
                                     lambda s, c: w2[s][:, WV, c * HP * DH:(c + 1) * HP * DH], C)

            def v_pair(m, i):
                v_one(2 * m, i)
                v_one(2 * m + 1, i).then_inc(proj_done, 1)

            def scores(a, u):
                j, t = u % HP, u // HP
                if u >= 2:
                    pe.wait_ge(biased, a * UNITS + (u - 1))
                for i in range(BU):
                    b = t * BU + i
                    mm = pe.matmul(score_ps[u % 2][:, i * S:(i + 1) * S], qt[:, j, b * S:(b + 1) * S], kt[:, j, b * S:(b + 1) * S],
                                   start=True, stop=True)
                mm.then_inc(scores_done, 1)

            def turn(a, u):
                pe.wait_ge(probs_done, a * UNITS + (u + 1))
                if u == 0:
                    pe.wait_ge(at_split, a * UNITS)
                for i in range(BU):
                    mm = pe.transpose(turn_ps[:, i * S:(i + 1) * S], probs[:, u, i, :], ident[:, :])
                mm.then_inc(turned, 1)

            def pv(a, u):
                j, t = u % HP, u // HP
                pe.wait_ge(turn_copied, a * UNITS + (u + 1))
                if isinstance(a, int) and a == LAST:
                    pe.wait_ge(at_split, a * UNITS + u)
                elif u >= 2:
                    pe.wait_ge(at_split, a * UNITS + (u - 1))
                for i in range(BU):
                    b = t * BU + i
                    mm = pe.matmul(pv_bank(a, u)[:, i * S:(i + 1) * S], v_sb[:, b, j * DH:(j + 1) * DH], probs_t[:, u % 2, i, :],
                                   start=True, stop=True)
                mm.then_inc(pv_done, 1)

            def out_proj(p, b, opens=False):
                pe.wait_ge(at_split, p * UNITS - (HP if b < BU else 0))
                if b < BANKS:
                    pe.wait_ge(proj_copied, p * PROJ + (QK + b + 1))
                else:
                    pe.wait_ge(acc_done, p * B + (b + 1 - BANKS))
                mm = split_product(proj_ps[b % BANKS][:, :], lambda s, j: at2[s][:, j, b * P:(b + 1) * P],
                                   lambda s, j: w2[s][:, WO, j * D:(j + 1) * D], HP, stop=not opens)
                mm.then_inc(first_share if opens else out_done, 1)

            def last_out(b):
                pe.wait_ge(at_split, NPH * UNITS - (HP if b < BU else 0))
                mm = split_product(proj_ps[b % BANKS][:, :], lambda s, j: at_last[s][:, j, b * P:(b + 1) * P],
                                   lambda s, j: wo_last[s][:, j * D:(j + 1) * D], HP, start=False)
                mm.then_inc(out_done, 1)

            def turn_xn(i):
                pe.wait_ge(xn_done, i + 1)
                if i >= G:
                    pe.wait_ge(xt_lo_done, i - G + 1)
                for c in range(C):
                    mm = pe.transpose(xn_ps[i % G][:, c * P:(c + 1) * P], xn[:, i % G, c * P:(c + 1) * P], ident[:, :])
                mm.then_inc(xt_turned, 1)

            def k_pieces(t):
                def wait(c):
                    if t == 0 and c == 0:
                        pe.wait_ge(wk_half_lo, 1)
                    if t == 0 and c == 2:
                        pe.wait_ge(w_lo_done[WK], 1)
                    pe.wait_ge(ctx_lo_done, t * C + c + 1)
                return wait

            for m in range(UNITS):
                q_or_k(2 * m + 1, m, k_pieces(m // HP) if m % HP == 0 else None)
            pe.wait_ge(ident_done, 1)
            pe.wait_ge(w_lo_done[WV], 1)
            for m in range(3):
                pe.wait_ge(proj_copied, m + 1)
                v_one(2 * m, m)
                if m == 2:
                    turn_xn(0)
                    turn_xn(1)
                v_one(2 * m + 1, m).then_inc(proj_done, 1)
            turn_xn(2)
            turn_xn(3)
            pe.wait_ge(proj_copied, UNITS)
            v_one(6, 3)
            pe.wait_ge(w_lo_done[WQ], 1)
            pe.wait_ge(xt_lo_done, G)
            pe.wait_ge(proj_copied, UNITS + 1)
            q_or_k(0, 0)
            turn_xn(4)
            turn_xn(5)

            def turn_rows(c):
                if c == 2:
                    turn_xn(6)
                    turn_xn(7)

            pe.wait_ge(proj_copied, UNITS + 2)
            q_or_k(2, 1, turn_rows)
            pe.wait_ge(proj_copied, UNITS + 3)
            pe.wait_ge(xt_lo_done, B)
            q_or_k(4, 2)
            pe.wait_ge(proj_copied, UNITS + 4)
            q_or_k(6, 0)
            v_one(7, 3).then_inc(proj_done, 1)

            def iteration(p):
                a = p - 1

                def chunk(n):
                    if n < BANKS:
                        pe.wait_ge(acc_done, (p - 1) * B + (B - BANKS + n + 1))
                    else:
                        pe.wait_ge(proj_copied, p * PROJ + (n - BANKS + 1))
                    if n == 0:
                        pe.wait_ge(w_lo_done[WQ], p + 1)
                    if n == 1:
                        pe.wait_ge(w_lo_done[WK], p + 1)
                    if n == QK:
                        pe.wait_ge(w_lo_done[WV], p + 1)
                    return q_or_k(n, n % BANKS) if n < QK else v_pair(n - QK, n % BANKS)

                pe.wait_ge(proj_copied, p * PROJ - 1)
                scores(a, 0)
                scores(a, 1)
                chunk(0)
                chunk(1)
                scores(a, 2)
                chunk(2)
                scores(a, 3)
                pe.wait_ge(proj_copied, p * PROJ)
                chunk(3)
                pv(a, 0)
                chunk(4)
                chunk(5)
                pv(a, 1)
                chunk(6)
                chunk(7)
                if isinstance(p, int):
                    return chunk
                chunk(QK)
                pv(a, 2)
                chunk(QK + 1)
                pv(a, 3)
                chunk(QK + 2)
                chunk(QK + 3)
                pe.wait_ge(w_lo_done[WO], p)
                for b in range(B):
                    out_proj(p, b)

            with pe.Fori(1, LAST) as p:
                iteration(p)

            chunk = iteration(LAST)
            chunk(QK)
            pv(LAST - 1, 2)
            pe.wait_ge(proj_copied, LAST * PROJ + QK)
            scores(LAST, 0)
            chunk(QK + 1)
            pv(LAST - 1, 3)
            scores(LAST, 1)
            chunk(QK + 2)
            turn(LAST, 0)
            chunk(QK + 3)
            scores(LAST, 2)
            pe.wait_ge(proj_copied, NPH * PROJ)
            pv(LAST, 0)
            pe.wait_ge(w_lo_done[WO], LAST)
            out_proj(LAST, 0, True)
            turn(LAST, 1)
            out_proj(LAST, 1, True)
            scores(LAST, 3)
            pv(LAST, 1)
            out_proj(LAST, 2, True)
            out_proj(LAST, 3, True)
            turn(LAST, 2)
            pe.wait_ge(w_lo_done[WO], NPH)
            last_out(0)
            pv(LAST, 2)
            last_out(1)
            turn(LAST, 3)
            last_out(2)
            pv(LAST, 3)
            last_out(3)
            for b in range(BANKS, B):
                out_proj(LAST, b, True)

            def turn_xf(i):
                pe.wait_ge(xf_done, i + 1)
                if i >= 2:
                    pe.wait_ge(xf_lo_done, i - 1)
                for c in range(C):
                    mm = pe.transpose(score_ps[i % 2][:, c * P:(c + 1) * P], xf[:, i % G, c * P:(c + 1) * P], ident[:, :])
                mm.then_inc(xf_turned, 1)

            def rows(i):
                return lambda s, c: xt2[s][:, c, i * P:(i + 1) * P]

            def logits(i):
                pe.wait_ge(xf_lo_done, i + 1)
                if i >= G:
                    pe.wait_ge(hg_done, G)
                else:
                    pe.wait_ge(at_split, NPH * UNITS)
                split_product(lg_ps(i), rows(i), lambda s, c: lg_w[s][:, c, :], C).then_inc(logits_done, 1)

            def base(i):
                if i >= 3:
                    pe.wait_ge(final_done, i - 2)
                else:
                    pe.wait_ge(acc_done, B * LAST + BANKS + i + 1)
                pe.wait_ge(xf_lo_done, i + 1)
                o = proj_ps[i % 3][:, :]
                for c in range(C):
                    for m, (l, r) in enumerate(((0, 0), (1, 0), (0, 1))):
                        pe.matmul(o, rows(i)(l, c), base_w[r][:, c, :], start=(c == 0 and m == 0), stop=False)

            def turn_hg(n):
                pe.wait_ge(hg_done, 2 * n + 2)
                if n:
                    pe.wait_ge(hg_lo_done, n)
                for i in range(2):
                    for e in range(2):
                        mm = pe.transpose(hgt_ps[:, i, e, :], hg[:, (2 * n + i) % G, e * ERH:(e + 1) * ERH], ident[:, :])
                mm.then_inc(hg_turned, 1)

            def lora(i):
                pe.wait_ge(hg_lo_done, i // 2 + 1)
                o = proj_ps[i % 3][:, :]
                for e in range(2):
                    for m, (l, r) in enumerate(((0, 0), (1, 0), (0, 1))):
                        mm = pe.matmul(o, (hgt_hi, hgt_lo)[l][:, i % 2, e, :], lb_w[r][:, e, :], start=False, stop=(e == 1 and m == 2))
                mm.then_inc(ffn_done, 1)

            last_out(4)
            turn_xf(0)
            turn_xf(1)
            last_out(5)
            turn_xf(2)
            turn_xf(3)
            for k in (WQ, WK, WV):
                pe.wait_ge(w_lo_done[k], NPH + 1)
            last_out(6)
            last_out(7)
            for i in range(G):
                logits(i)
            base(0)
            base(1)
            turn_xf(4)
            turn_xf(5)
            base(2)
            turn_xf(6)
            turn_xf(7)
            turn_hg(0)
            for i in range(G, B):
                logits(i)
            pe.wait_ge(w_lo_done[WO], NPH + 1)
            lora(0)
            lora(1)
            turn_hg(1)
            base(3)
            lora(2)
            lora(3)
            base(4)
            base(5)
            turn_hg(2)
            base(6)
            lora(4)
            lora(5)
            turn_hg(3)
            base(7)
            lora(6)
            lora(7)


def kernel(**inputs):
    import numpy as np
    import concourse.bacc as bacc
    from concourse.bass_utils import run_bass_kernel_spmd

    a = {k: np.asarray(v) for k, v in inputs.items()}

    def by_phase(w):
        return w.reshape(NPH, HP, DH, C, P).transpose(0, 4, 3, 1, 2).reshape(NPH, P, WN)

    weights = np.zeros((NPH + 1, 4, P, WN), np.float32)
    for k, name in ((WQ, "w_q"), (WK, "w_k"), (WV, "w_v")):
        weights[:NPH, k] = by_phase(a["L0_xattn_" + name])
    weights[:NPH, WO] = a["L0_xattn_w_out"].reshape(D, NPH, HP, DH).transpose(1, 3, 2, 0).reshape(NPH, P, HP * D)
    base = a["L0_ffn_base_W"].T.reshape(C, P, D).transpose(1, 0, 2).reshape(P, 2, WN)
    weights[NPH, 0:2] = base.transpose(1, 0, 2)
    lg = np.zeros((D, LG), np.float32)
    lg[:, :ER] = a["L0_ffn_lora_A"].reshape(ER, D).T
    lg[:, ER:ER + E] = a["L0_ffn_gate_W"].T
    weights[NPH, 2] = lg.reshape(C, P, LG).transpose(1, 0, 2).reshape(P, WN)
    lb = a["L0_ffn_lora_B"].transpose(0, 2, 1).reshape(2, ERH, D)
    weights[NPH, 3, :ERH] = lb.transpose(1, 0, 2).reshape(ERH, WN)

    arrays = {
        "x": a["x"],
        "ctx_t": np.ascontiguousarray(a["ctx_4096"].reshape(T, D).T).reshape(C, P, T),
        "weights": weights,
        "bias": np.ascontiguousarray(a["L0_xattn_position_bias"].reshape(NPH, HP, S, S).transpose(0, 2, 1, 3)),
        "mask": np.ascontiguousarray(a["mask_BxSxS2_bk0"]),
        "g_x": a["g_xattn"], "g_f": a["g_ffn"], "ln_w": a["L0_xattn_ln_weight"],
    }
    nc = bacc.Bacc("TRN2", target_bir_lowering=False, num_devices=1)
    args = [nc.dram_tensor("in_" + n, v.shape, mybir.dt.from_np(v.dtype), kind="ExternalInput").ap() for n, v in arrays.items()]
    out = nc.dram_tensor("out", (B, S, D), F32, kind="ExternalOutput").ap()
    build(nc, *args, out)
    r = run_bass_kernel_spmd(nc, [{"in_" + n: v for n, v in arrays.items()}], core_ids=[0])
    return r.results[0]["out"]
```
